# Optimizing a Trainium2 kernel written in Bass

```python
import numpy as np
import jax
import jax.numpy as jnp

def _softmax(x, axis=-1):
    return jax.nn.softmax(x, axis=axis)

def _gelu(x):
    return jax.nn.gelu(x, approximate=True)

def _silu(x):
    return jax.nn.silu(x)

def _sigmoid(x):
    return jax.nn.sigmoid(x)

def _layernorm(x, axis=-1, eps=1e-05):
    m = jnp.mean(x, axis=axis, keepdims=True)
    v = jnp.var(x, axis=axis, keepdims=True)
    return (x - m) / jnp.sqrt(v + eps)

def _scatter_add(tgt, idx, src, axis=0):
    return tgt.at[idx].add(src)

def _segment_sum(src, seg, n):
    return jax.ops.segment_sum(src, seg, n)
kernel_name = 'mk_seq_preln_d1_jaxref_r8_27410b'

def setup_inputs(seed: int=0):
    np.random.seed(seed)
    _w = jnp.asarray

    def _L0_attn_setup():
        import jax, jax.numpy as jnp
        import numpy as np
        D_MODEL = 256
        D_STATE = 128
        D_CONV = 4
        EXPAND = 2
        HEADDIM = 64
        D_INNER = EXPAND * D_MODEL
        NHEADS = D_INNER // HEADDIM
        CONV_DIM = D_INNER + 2 * D_STATE
        IN_PROJ = 2 * D_INNER + 2 * D_STATE + NHEADS
        INTER = 704
        EPS = 1e-06
        CHUNK = 128

        def rmsnorm(x, w, eps=EPS):
            var = jnp.mean(jnp.square(x), axis=-1, keepdims=True)
            return x * jax.lax.rsqrt(var + eps) * w

        def dw_causal_conv(x, w, b):
            xt = jnp.transpose(x, (0, 2, 1))
            xt = jnp.pad(xt, ((0, 0), (0, 0), (D_CONV - 1, 0)))
            y = jax.lax.conv_general_dilated(xt, w[:, None, :], window_strides=(1,), padding='VALID', feature_group_count=w.shape[0], dimension_numbers=('NCH', 'OIH', 'NCH'))
            y = y + b[None, :, None]
            return jnp.transpose(y, (0, 2, 1))

        def segsum(x):
            T = x.shape[-1]
            xx = jnp.broadcast_to(x[..., None], (*x.shape, T))
            xx = jnp.where(jnp.tril(jnp.ones((T, T), bool), -1), xx, 0.0)
            s = jnp.cumsum(xx, axis=-2)
            return jnp.where(jnp.tril(jnp.ones((T, T), bool), 0), s, -jnp.inf)

        def ssd(x, dt, A, Bm, Cm):
            b, l, h, p = x.shape
            n = Bm.shape[-1]
            c = l // CHUNK
            xr = x.reshape(b, c, CHUNK, h, p)
            dtr = dt.reshape(b, c, CHUNK, h)
            Br = Bm.reshape(b, c, CHUNK, n)
            Cr = Cm.reshape(b, c, CHUNK, n)
            dA = jnp.transpose(dtr * A, (0, 3, 1, 2))
            A_cum = jnp.cumsum(dA, axis=-1)
            L = jnp.exp(segsum(dA))
            xdt = xr * dtr[..., None]
            Y_diag = jnp.einsum('bcln,bcsn,bhcls,bcshp->bclhp', Cr, Br, L, xdt)
            decay_states = jnp.exp(A_cum[..., -1:] - A_cum)
            states = jnp.einsum('bcln,bhcl,bclhp->bchpn', Br, decay_states, xdt)
            A_last = A_cum[..., -1]
            decay_chunk = jnp.exp(segsum(jnp.pad(A_last, ((0, 0), (0, 0), (1, 0)))))
            states_cat = jnp.concatenate([jnp.zeros_like(states[:, :1]), states], axis=1)
            new_states = jnp.einsum('bhzc,bchpn->bzhpn', decay_chunk, states_cat)
            prev = new_states[:, :-1]
            state_decay = jnp.exp(A_cum)
            Y_off = jnp.einsum('bcln,bchpn,bhcl->bclhp', Cr, prev, state_decay)
            return (Y_diag + Y_off).reshape(b, l, h, p)
        key = jax.random.key(seed)
        ks = jax.random.split(key, 10)
        B, L = (2, 256)
        s = 0.02
        return {'hidden_states': jax.random.normal(ks[0], (B, L, D_MODEL), jnp.float32), 'norm1_w': jnp.ones((D_MODEL,), jnp.float32), 'in_proj_w': jax.random.normal(ks[1], (D_MODEL, IN_PROJ), jnp.float32) * s, 'conv_w': jax.random.normal(ks[2], (CONV_DIM, D_CONV), jnp.float32) * 0.1, 'conv_b': jnp.zeros((CONV_DIM,), jnp.float32), 'dt_bias': jax.random.uniform(ks[3], (NHEADS,), jnp.float32, -4.0, -1.0), 'A_log': jnp.log(jnp.arange(1, NHEADS + 1, dtype=jnp.float32)), 'D_param': jnp.ones((NHEADS,), jnp.float32), 'mixer_norm_w': jnp.ones((D_INNER,), jnp.float32), 'out_proj_w': jax.random.normal(ks[4], (D_INNER, D_MODEL), jnp.float32) * s, 'norm2_w': jnp.ones((D_MODEL,), jnp.float32), 'gate_w': jax.random.normal(ks[5], (D_MODEL, INTER), jnp.float32) * s, 'up_w': jax.random.normal(ks[6], (D_MODEL, INTER), jnp.float32) * s, 'down_w': jax.random.normal(ks[7], (INTER, D_MODEL), jnp.float32) * s}
    _L0_attn_in = _L0_attn_setup()

    def _L0_ffn_setup():
        import jax, jax.numpy as jnp
        import numpy as np
        E = 8
        TOP_K = 2
        D = 256
        M = 896
        B, S = (2, 256)
        key = jax.random.key(seed)
        kx, kg, k1, k2, k3 = jax.random.split(key, 5)
        x = jax.random.normal(kx, (B, S, D), dtype=jnp.float32)
        gate_w = jax.random.normal(kg, (D, E), dtype=jnp.float32) / np.sqrt(D)
        w1 = jax.random.normal(k1, (E, D, M), dtype=jnp.float32) / np.sqrt(D)
        w2 = jax.random.normal(k2, (E, M, D), dtype=jnp.float32) / np.sqrt(M)
        w3 = jax.random.normal(k3, (E, D, M), dtype=jnp.float32) / np.sqrt(D)
        return {'x': x, 'gate_w': gate_w, 'w1': w1, 'w2': w2, 'w3': w3}
    _L0_ffn_in = _L0_ffn_setup()
    _d = {'L0_attn_hidden_states': _L0_attn_in['hidden_states'], 'L0_attn_norm1_w': _L0_attn_in['norm1_w'], 'L0_attn_in_proj_w': _L0_attn_in['in_proj_w'], 'L0_attn_conv_w': _L0_attn_in['conv_w'], 'L0_attn_conv_b': _L0_attn_in['conv_b'], 'L0_attn_dt_bias': _L0_attn_in['dt_bias'], 'L0_attn_A_log': _L0_attn_in['A_log'], 'L0_attn_D_param': _L0_attn_in['D_param'], 'L0_attn_mixer_norm_w': _L0_attn_in['mixer_norm_w'], 'L0_attn_out_proj_w': _L0_attn_in['out_proj_w'], 'L0_attn_norm2_w': _L0_attn_in['norm2_w'], 'L0_attn_gate_w': _L0_attn_in['gate_w'], 'L0_attn_up_w': _L0_attn_in['up_w'], 'L0_attn_down_w': _L0_attn_in['down_w'], 'L0_ffn_gate_w': _L0_ffn_in['gate_w'], 'L0_ffn_w1': _L0_ffn_in['w1'], 'L0_ffn_w2': _L0_ffn_in['w2'], 'L0_ffn_w3': _L0_ffn_in['w3']}
    _x0 = _d['L0_attn_hidden_states']
    _d['L0_attn_hidden_states'] = jax.random.normal(jax.random.fold_in(jax.random.key(seed), 1), (4, 512, 256), dtype=_x0.dtype)
    del _x0
    return _d

def reference(L0_attn_hidden_states, L0_attn_norm1_w, L0_attn_in_proj_w, L0_attn_conv_w, L0_attn_conv_b, L0_attn_dt_bias, L0_attn_A_log, L0_attn_D_param, L0_attn_mixer_norm_w, L0_attn_out_proj_w, L0_attn_norm2_w, L0_attn_gate_w, L0_attn_up_w, L0_attn_down_w, L0_ffn_gate_w, L0_ffn_w1, L0_ffn_w2, L0_ffn_w3):

    def _L0_attn_ref(hidden_states, norm1_w, in_proj_w, conv_w, conv_b, dt_bias, A_log, D_param, mixer_norm_w, out_proj_w, norm2_w, gate_w, up_w, down_w):
        import jax, jax.numpy as jnp
        import numpy as np
        D_MODEL = 256
        D_STATE = 128
        D_CONV = 4
        EXPAND = 2
        HEADDIM = 64
        D_INNER = EXPAND * D_MODEL
        NHEADS = D_INNER // HEADDIM
        CONV_DIM = D_INNER + 2 * D_STATE
        IN_PROJ = 2 * D_INNER + 2 * D_STATE + NHEADS
        INTER = 704
        EPS = 1e-06
        CHUNK = 128

        def rmsnorm(x, w, eps=EPS):
            var = jnp.mean(jnp.square(x), axis=-1, keepdims=True)
            return x * jax.lax.rsqrt(var + eps) * w

        def dw_causal_conv(x, w, b):
            xt = jnp.transpose(x, (0, 2, 1))
            xt = jnp.pad(xt, ((0, 0), (0, 0), (D_CONV - 1, 0)))
            y = jax.lax.conv_general_dilated(xt, w[:, None, :], window_strides=(1,), padding='VALID', feature_group_count=w.shape[0], dimension_numbers=('NCH', 'OIH', 'NCH'))
            y = y + b[None, :, None]
            return jnp.transpose(y, (0, 2, 1))

        def segsum(x):
            T = x.shape[-1]
            xx = jnp.broadcast_to(x[..., None], (*x.shape, T))
            xx = jnp.where(jnp.tril(jnp.ones((T, T), bool), -1), xx, 0.0)
            s = jnp.cumsum(xx, axis=-2)
            return jnp.where(jnp.tril(jnp.ones((T, T), bool), 0), s, -jnp.inf)

        def ssd(x, dt, A, Bm, Cm):
            b, l, h, p = x.shape
            n = Bm.shape[-1]
            c = l // CHUNK
            xr = x.reshape(b, c, CHUNK, h, p)
            dtr = dt.reshape(b, c, CHUNK, h)
            Br = Bm.reshape(b, c, CHUNK, n)
            Cr = Cm.reshape(b, c, CHUNK, n)
            dA = jnp.transpose(dtr * A, (0, 3, 1, 2))
            A_cum = jnp.cumsum(dA, axis=-1)
            L = jnp.exp(segsum(dA))
            xdt = xr * dtr[..., None]
            Y_diag = jnp.einsum('bcln,bcsn,bhcls,bcshp->bclhp', Cr, Br, L, xdt)
            decay_states = jnp.exp(A_cum[..., -1:] - A_cum)
            states = jnp.einsum('bcln,bhcl,bclhp->bchpn', Br, decay_states, xdt)
            A_last = A_cum[..., -1]
            decay_chunk = jnp.exp(segsum(jnp.pad(A_last, ((0, 0), (0, 0), (1, 0)))))
            states_cat = jnp.concatenate([jnp.zeros_like(states[:, :1]), states], axis=1)
            new_states = jnp.einsum('bhzc,bchpn->bzhpn', decay_chunk, states_cat)
            prev = new_states[:, :-1]
            state_decay = jnp.exp(A_cum)
            Y_off = jnp.einsum('bcln,bchpn,bhcl->bclhp', Cr, prev, state_decay)
            return (Y_diag + Y_off).reshape(b, l, h, p)
        B, L, _ = hidden_states.shape
        res = hidden_states
        h = rmsnorm(hidden_states, norm1_w)
        zxbcdt = h @ in_proj_w
        z = zxbcdt[..., :D_INNER]
        xBC = zxbcdt[..., D_INNER:D_INNER + CONV_DIM]
        dt = jax.nn.softplus(zxbcdt[..., -NHEADS:] + dt_bias)
        xBC = jax.nn.silu(dw_causal_conv(xBC, conv_w, conv_b))
        xs = xBC[..., :D_INNER].reshape(B, L, NHEADS, HEADDIM)
        Bm = xBC[..., D_INNER:D_INNER + D_STATE]
        Cm = xBC[..., D_INNER + D_STATE:]
        A = -jnp.exp(A_log)
        y = ssd(xs, dt, A, Bm, Cm)
        y = y + D_param[None, None, :, None] * xs
        y = y.reshape(B, L, D_INNER)
        y = rmsnorm(y * jax.nn.silu(z), mixer_norm_w)
        h1 = res + y @ out_proj_w
        h2 = rmsnorm(h1, norm2_w)
        mlp = jax.nn.silu(h2 @ gate_w) * (h2 @ up_w) @ down_w
        return h1 + mlp

    def _L0_ffn_ref(x, gate_w, w1, w2, w3):
        import jax, jax.numpy as jnp
        import numpy as np
        E = 8
        TOP_K = 2
        D = 256
        M = 896
        B, S = (2, 256)
        b, s, d = x.shape
        x_flat = x.reshape(-1, d)
        router_logits = x_flat @ gate_w
        router_probs = jax.nn.softmax(router_logits, axis=-1)
        topk_w, topk_idx = jax.lax.top_k(router_probs, TOP_K)
        topk_w = topk_w / jnp.sum(topk_w, axis=-1, keepdims=True)
        idx_flat = topk_idx.reshape(-1)
        sort_idx = jnp.argsort(idx_flat)
        x_rep_sort = jnp.take(x_flat, sort_idx // TOP_K, axis=0)
        group_sizes = jnp.bincount(idx_flat, length=E).astype(jnp.int32)
        h = jax.lax.ragged_dot(x_rep_sort, w1, group_sizes)
        h = jax.nn.silu(h) * jax.lax.ragged_dot(x_rep_sort, w3, group_sizes)
        out_sort = jax.lax.ragged_dot(h, w2, group_sizes)
        inv_sort_idx = jnp.argsort(sort_idx)
        out_rep = jnp.take(out_sort, inv_sort_idx, axis=0).reshape(-1, TOP_K, d)
        out = jnp.einsum('tkd,tk->td', out_rep, topk_w)
        return out.reshape(b, s, d)
    x = L0_attn_hidden_states
    x = x + _L0_attn_ref(_layernorm(x, axis=-1), L0_attn_norm1_w, L0_attn_in_proj_w, L0_attn_conv_w, L0_attn_conv_b, L0_attn_dt_bias, L0_attn_A_log, L0_attn_D_param, L0_attn_mixer_norm_w, L0_attn_out_proj_w, L0_attn_norm2_w, L0_attn_gate_w, L0_attn_up_w, L0_attn_down_w)
    x = x + _L0_ffn_ref(_layernorm(x, axis=-1), L0_ffn_gate_w, L0_ffn_w1, L0_ffn_w2, L0_ffn_w3)
    return x

_drawn_inputs = setup_inputs


def setup_inputs(seed=0):
    import zlib

    import numpy as np

    out = dict(_drawn_inputs(seed))
    spreads = {'L0_attn_norm1_w': (1.0, 0.2),
     'L0_attn_conv_b': (0.0, 0.1),
     'L0_attn_D_param': (1.0, 0.2),
     'L0_attn_mixer_norm_w': (1.0, 0.2),
     'L0_attn_norm2_w': (1.0, 0.6)}
    factors = {'L0_attn_dt_bias': 8.0, 'L0_attn_A_log': 7.854}
    for name, (base, spread) in spreads.items():
        noise = np.random.default_rng([zlib.crc32(name.encode()), seed]).standard_normal(out[name].shape)
        drawn = base * np.exp(spread * noise) if base else spread * noise
        out[name] = jnp.asarray(drawn.astype(out[name].dtype))
    for name, factor in factors.items():
        out[name] = (out[name] * factor).astype(out[name].dtype)
    return out
```

```python
from contextlib import ExitStack

import numpy as np

import concourse.bass as bass
from concourse import mybir

P = 128
SEQS, SEQ = 4, 512
TOKENS = SEQS * SEQ
CH = SEQ // P
D = 256
KD = D // P
INNER = 512
HEADS, HD = 8, 64
STATE = 128
CONV = INNER + 2 * STATE
CB = CONV // P
TAPS = 4
PROJ = 2 * INNER + 2 * STATE + HEADS
INTER = 704
JB = -(-INTER // P)
E, TOP = 8, 2
M = 896
MB = M // P
HALF = M // 2
TILES = TOKENS * TOP // P + E - 1
LIST = TOKENS // P
SLOT_TILES = E * LIST + TILES - E - LIST + 1
EXPERT = 2 * KD * M + MB * D
EARLY = 2
LN_EPS, RMS_EPS = 1e-5, 1e-6
SERIES = 8

F32 = mybir.dt.float32
I32 = mybir.dt.int32
ALU = mybir.AluOpType
ACT = mybir.ActivationFunctionType
AX = mybir.AxisListType.X

C_ID, C_UPTO, C_AFTER, C_BEFORE, C_ONES = 0, P, 2 * P, 3 * P, 4 * P
C_RANK = 5 * P
C_LISTS = C_RANK + E
C_FULL = C_LISTS + E
C_TILE = C_FULL + LIST
C_ROW = C_TILE + TILES
C_TOKEN = C_ROW + 1
C_POW = C_TOKEN + SEQS * CH
N_CONST = C_POW + 4
V_N1, V_MN, V_N2 = 0, KD, KD + 4
V_CW = V_N2 + KD
V_CB = V_CW + CB * TAPS
V_DTB = V_CB + CB
V_ALOG = V_DTB + HEADS
V_D = V_ALOG + HEADS
N_VEC = V_D + HEADS


def constants():
    c = np.zeros((P, N_CONST), np.float32)
    r = np.arange(P)
    c[:, C_ID:C_ID + P] = np.eye(P)
    c[:, C_UPTO:C_UPTO + P] = r[:, None] <= r[None, :]
    c[:, C_AFTER:C_AFTER + P] = r[:, None] > r[None, :]
    c[:, C_BEFORE:C_BEFORE + P] = r[:, None] < r[None, :]
    c[:, C_ONES:C_ONES + P] = 1.0
    c[:, C_RANK:C_RANK + E] = E - np.arange(E)
    c[:, C_LISTS:C_LISTS + E] = TOKENS * np.arange(E)
    c[:, C_FULL:C_FULL + LIST] = P * np.arange(LIST)
    c[:, C_TILE:C_TILE + TILES] = np.arange(TILES)
    c[:, C_ROW] = r
    c[:, C_TOKEN:C_TOKEN + SEQS * CH] = r[:, None] + P * np.arange(SEQS * CH)
    c[:, C_POW:C_POW + 4] = -0.5
    empty = np.zeros((SLOT_TILES, P, 2), np.float32)
    empty[:, :, 0] = TOKENS + r
    return c, empty.reshape(SLOT_TILES * P, 2)


class Steps:

    def __init__(self, eng, sem, length):
        self.eng, self.sem, self.length = eng, sem, length

    def start(self, n):
        self.n, self.k = n, 0

    def then(self, ins):
        self.k += 1
        assert self.k <= self.length
        ins.then_inc(self.sem, 1)
        self.eng.wait_ge(self.sem, self.n * self.length + self.k)

    def end(self):
        assert self.k == self.length, (self.k, self.length)


def nth(n, per, k):
    return n * per + (k + 1)


def build(nc, hidden, vecs, consts, empty, in_proj, out_proj, gate_w, up_w, down_w,
          router_w, w1, w2, w3, out):
    xn_rows = nc.dram_tensor("xn_rows", [TOKENS + P, D], F32).ap()
    lists = nc.dram_tensor("lists", [SLOT_TILES * P, 2], F32).ap()

    ctx = ExitStack()
    with ctx:
        def sem(name):
            return ctx.enter_context(nc.semaphore(name))

        COLS = 53200
        big = ctx.enter_context(nc.sbuf_tensor("big", [P, COLS], F32))
        at = [EARLY * EXPERT]

        def cols(*shape):
            n = int(np.prod(shape))
            a = at[0]
            at[0] += n
            assert at[0] <= COLS, at[0]
            v = big[:, a:a + n]
            if len(shape) == 2:
                v = v.rearrange("p (a b) -> p a b", b=shape[1])
            if len(shape) == 3:
                v = v.rearrange("p (a b c) -> p a b c", b=shape[1], c=shape[2])
            return v

        win = cols(KD, PROJ)
        wout = cols(4, D)
        h = cols(CH, D)
        hT = cols(KD, SEQ)
        xc = cols(CB, SEQ)
        sz = cols(CH, INNER)
        xs = cols(INNER)
        xdt = cols(2, INNER)
        xdtd = cols(2, INNER)
        xsd = cols(2, INNER)
        bg = cols(2, 2 * P)
        gm = cols(2, P)
        mda = cols(2, HEADS * P)
        em = cols(2, HEADS * P)
        yb = cols(2, INNER)
        yTs = cols(4, P)
        st = cols(INNER)
        ab = cols(D)
        junk_y = cols(INNER)
        SOON = at[0] // EXPERT
        wgate = cols(KD, INTER)
        wup = cols(KD, INTER)
        wdown = cols(JB, D)
        x = cols(SEQS * CH, D)
        h1 = cols(CH, D)
        h2T = cols(KD, SEQ)
        sg = cols(2, SEQ)
        hid = cols(JB, SEQ)
        xn = cols(CH, D)
        xnT = cols(KD, P)
        junk_h = cols(D)
        dec = cols(3, CH, HEADS)
        dtx, dta, dtu, dtd, dtr, dts, dts2, dtq, dtp, dtl, dtv, dA = (cols(CH, HEADS) for _ in range(12))
        st6 = cols(CH, 6)
        mv = cols(CH, 2)
        ve, rs, rr, t4a, t4b, cur_rs, ssy, ry, vy, ssh, rh, vh, ve2, rs2 = (cols(CH) for _ in range(14))
        cur_mv = cols(CH, 2)
        st6b = cols(CH, 6)
        mv2 = cols(CH, 2)
        late_end = at[0]

        at[0] = E * EXPERT
        moe_small = at[0]
        xg = cols(KD * P)
        xT = cols(KD, P)
        sa = cols(2, HALF)
        ha = cols(MB, P)
        hTs = cols(MB, P)
        ys = cols(D)
        at[0] = max(at[0], late_end)
        cst = cols(N_CONST)
        vec = cols(N_VEC)
        wr = cols(KD, E)
        aneg = cols(HEADS)
        zero = cols(D)
        lg, rd, re_, rp, req, rsc, o1, o2, rq, sel, rpos, radr, rt = (cols(CH, E) for _ in range(13))
        rmx, rsum, rrec, rm1, rm2, p1, p2, ps12, pr12 = (cols(CH) for _ in range(9))
        rec = cols(CH, TOP, 2)
        slotf = cols(CH, TOP)
        slot = cols(CH, TOP).bitcast(I32)
        run = cols(E)
        full = cols(E, LIST)
        nt = cols(E)
        upto = cols(E)
        ge = cols(E)
        gn = cols(E)
        ecol = cols(1)
        scol = cols(1)
        rcol = cols(1)
        ridx = cols(1).bitcast(I32)
        ge_row = cols(TILES, E)
        erowf = cols(TILES)
        erow = cols(TILES).bitcast(I32)
        recg = cols(2 * P)
        ids = cols(TILES).bitcast(I32)
        wts = cols(TILES)
        gidx = cols(1).bitcast(I32)
        sidx = cols(1).bitcast(I32)

        ident = cst[:, C_ID:C_ID + P]
        tri_upto = cst[:, C_UPTO:C_UPTO + P]
        tri_after = cst[:, C_AFTER:C_AFTER + P]
        tri_before = cst[:, C_BEFORE:C_BEFORE + P]
        ones = cst[:, C_ONES:C_ONES + P]

        def expert_cols(e, off, n):
            return big[:, bass.ds(e * EXPERT + off, n)]

        ps = ctx.enter_context(nc.psum_tensor("ps", [P, 8 * 512], F32))

        def bank(k, n=1):
            return ps[:, k * 512:(k + n) * 512]

        small_in, win_in, wout_in, wout_scaled, rest_in, x_first, x_rest = map(sem, ("small_in", "win_in", "wout_in", "wout_scaled", "rest_in", "x_first", "x_rest"))
        early_in, expert_in, lists_in, zeroed, pads_out = map(sem, ("early_in", "expert_in", "lists_in", "zeroed", "pads_out"))
        aneg_exp, aneg_ready, run_zero = map(sem, ("aneg_exp", "aneg_ready", "run_zero"))
        ln1_var, ln1_r, h_ready, hT_ps, hT0_taken, hT1_taken = map(sem, ("ln1_var", "ln1_r", "h_ready", "hT_ps", "hT0_taken", "hT1_taken"))
        cur_kept = sem("cur_kept")
        dt_ps, dt_taken, dt_abs, dt_exp, dA_ready, dec_ps, dec_taken = map(sem, ("dt_ps", "dt_taken", "dt_abs", "dt_exp", "dA_ready", "dec_ps", "dec_taken"))
        xbc_ps, tap_done, conv_taken, xc_ready = map(sem, ("xbc_ps", "tap_done", "conv_taken", "xc_ready"))
        z_ps, z_taken = map(sem, ("z_ps", "z_taken"))
        xs_ps, xs_taken, bg_ps, bg_taken, seg_ps, seg_taken = map(sem, ("xs_ps", "xs_taken", "bg_ps", "bg_taken", "seg_ps", "seg_taken"))
        mda_ready, xdt_ready, xdtd_ready, xsd_ready, em_ready = map(sem, ("mda_ready", "xdt_ready", "xdtd_ready", "xsd_ready", "em_ready"))
        off_ps, off_scaled, y_ps, y_taken, s_ps, s_taken, y3_ready, y4_ready, ssy_ready, ry_ready = map(sem, ("off_ps", "off_scaled", "y_ps", "y_taken", "s_ps", "s_taken", "y3_ready", "y4_ready", "ssy_ready", "ry_ready"))
        yT_ps, yT_taken, o_ps, o_taken, xh_ready, ssh_ready, rh_ready = map(sem, ("yT_ps", "yT_taken", "o_ps", "o_taken", "xh_ready", "ssh_ready", "rh_ready"))
        h2_ready, h2T_ps, h2T0_taken, h2T1_taken = map(sem, ("h2_ready", "h2T_ps", "h2T0_taken", "h2T1_taken"))
        gate_ps, gate_taken, up_ps, up_taken, down_ps, down_taken = map(sem, ("gate_ps", "gate_taken", "up_ps", "up_taken", "down_ps", "down_taken"))
        ln2_var, ln2_r, xn_ready, xn_out, x1_out = map(sem, ("ln2_var", "ln2_r", "xn_ready", "xn_out", "x1_out"))
        xnT_ps, xnT_taken, xnT1_taken, lg_ps, lg_taken = map(sem, ("xnT_ps", "xnT_taken", "xnT1_taken", "lg_ps", "lg_taken"))
        route_d, route_e, sel_ready, pos_ps, pos_taken, rec_ready, rec_out = map(sem, ("route_d", "route_e", "sel_ready", "pos_ps", "pos_taken", "rec_ready", "rec_out"))
        ridx_ready, erow_ready, recg_in, recT_ps, ids_ready = map(sem, ("ridx_ready", "erow_ready", "recg_in", "recT_ps", "ids_ready"))
        gidx_ready, sidx_ready, xg_in, xT_ps, xT_taken = map(sem, ("gidx_ready", "sidx_ready", "xg_in", "xT_ps", "xT_taken"))
        a_ps, a_taken, b_ps, b_taken, eT_ps, eT0_taken, eT1_taken, yd_ps, yd_taken, y_added = map(sem, ("a_ps", "a_taken", "b_ps", "b_taken", "eT_ps", "eT0_taken", "eT1_taken", "yd_ps", "yd_taken", "y_added"))
        ln1_step, dt_step, conv_step, gm_step, y_step, s_step, a_step, ln2_step, route_step, table_step = map(sem, ("ln1_step", "dt_step", "conv_step", "gm_step", "y_step", "s_step", "a_step", "ln2_step", "route_step", "table_step"))
        pool_ln1, pool_ry, pool_rh = map(sem, ("pool_ln1", "pool_ry", "pool_rh"))

        def over_seqs(eng, body):
            body(0, False, True)
            with eng.Fori(1, SEQS - 1) as b:
                body(b, True, True)
            body(SEQS - 1, True, False)

        block = ctx.enter_context(nc.Block())

        @block.sync
        def _(sp):
            xv = hidden.rearrange("(t p) d -> p t d", p=P)
            sp.dma_start(x[:, 0:CH, :], xv[:, 0:CH, :]).then_inc(x_first, 16)
            sp.dma_start(cst, consts).then_inc(small_in, 16)
            sp.dma_start(vec, vecs).then_inc(small_in, 16)
            sp.dma_start(win, in_proj.rearrange("(k p) n -> p k n", p=P)).then_inc(win_in, 16)
            sp.dma_start(wout, out_proj.rearrange("(k p) n -> p k n", p=P)).then_inc(wout_in, 16)
            sp.dma_start(x[:, CH:, :], xv[:, CH:, :]).then_inc(x_rest, 16)
            sp.dma_start(wgate, gate_w.rearrange("(k p) n -> p k n", p=P)).then_inc(rest_in, 16)
            sp.dma_start(wup, up_w.rearrange("(k p) n -> p k n", p=P)).then_inc(rest_in, 16)
            sp.dma_start(wdown[:, 0:JB - 1, :], down_w[0:(JB - 1) * P, :].rearrange("(k p) n -> p k n", p=P)).then_inc(rest_in, 16)
            sp.dma_start(wdown[0:INTER - (JB - 1) * P, JB - 1, :], down_w[(JB - 1) * P:INTER, :]).then_inc(rest_in, 16)
            sp.dma_start(wr, router_w.rearrange("(k p) n -> p k n", p=P)).then_inc(rest_in, 16)
            sp.dma_start(lists, empty).then_inc(lists_in, 16)
            sp.wait_ge(zeroed, 1)
            sp.dma_start(xn_rows[TOKENS:, :], zero).then_inc(pads_out, 16)
            sp.dma_start(out[TOKENS:, :], zero).then_inc(pads_out, 16)

            def load_expert(e, done):
                a = e * EXPERT
                for w, off in ((w1, 0), (w3, KD * M)):
                    sp.dma_start(big[:, a + off:a + off + KD * M].rearrange("p (k n) -> p k n", k=KD),
                                 w[e].rearrange("(k p) n -> p k n", p=P)).then_inc(done, 16)
                sp.dma_start(big[:, a + 2 * KD * M:a + EXPERT].rearrange("p (k n) -> p k n", k=MB),
                             w2[e].rearrange("(k p) n -> p k n", p=P)).then_inc(done, 16)

            def load_next(e):
                if e > EARLY:
                    sp.wait_ge(expert_in, 48 * (e - EARLY))
                load_expert(e, expert_in)

            for e in range(EARLY):
                load_expert(e, early_in)
            x1_rows = out[0:TOKENS, :].rearrange("(t p) d -> p t d", p=P)
            xn_tiles = xn_rows[0:TOKENS, :].rearrange("(t p) d -> p t d", p=P)

            def body(b, prev, nxt):
                sp.wait_ge(down_taken, nth(b, CH, CH - 1))
                sp.dma_start(x1_rows[:, bass.ds(b * CH, CH), :], x[:, bass.ds(b * CH, CH), :]).then_inc(x1_out, 16)
                sp.wait_ge(xn_ready, nth(b, 1, 0))
                sp.dma_start(xn_tiles[:, bass.ds(b * CH, CH), :], xn).then_inc(xn_out, 16)

            body(0, False, True)
            with sp.Fori(1, SEQS - 1) as b:
                body(b, True, True)
            sp.wait_ge(o_taken, SEQS * CH)
            sp.wait_ge(ssy_ready, SEQS * CH)
            for e in range(EARLY, SOON):
                load_next(e)
            body(SEQS - 1, True, False)
            sp.wait_ge(x1_out, 16 * SEQS)
            sp.wait_ge(xn_out, 16 * SEQS)
            sp.wait_ge(lg_ps, SEQS)
            sp.wait_ge(xg_in, 16 * 2)
            for e in range(SOON, E):
                load_next(e)
            sp.wait_ge(pads_out, 32)
            sp.wait_ge(lists_in, 16)

        @block.tensor
        def _(pe):
            mm = nc.tensor.matmul

            def transposed(out_ap, in_ap, n=P):
                return nc.tensor.transpose(out_ap, in_ap, ident[0:n, 0:n])

            def hT_(n):
                pe.wait_ge(h_ready, nth(n, 1, 0))
                for k in range(KD):
                    for t in range(CH):
                        last = transposed(bank(2 + k)[:, t * P:(t + 1) * P], h[:, t, k * P:(k + 1) * P])
                    last.then_inc(hT_ps, 1)

            def dt_(n):
                pe.wait_ge(hT0_taken, nth(n, 1, 0))
                pe.wait_ge(hT1_taken, nth(n, 1, 0))
                for t in range(CH):
                    for k in range(KD):
                        last = mm(bank(1)[:, t * HEADS:(t + 1) * HEADS], hT[:, k, t * P:(t + 1) * P],
                                  win[:, k, PROJ - HEADS:PROJ], start=(k == 0), stop=(k == KD - 1))
                last.then_inc(dt_ps, 1)

            def dec_(n):
                pe.wait_ge(dA_ready, nth(n, 1, 0))
                for i, tri in enumerate((tri_after, tri_upto, ones)):
                    last = mm(bank(1)[:, i * CH * HEADS:(i + 1) * CH * HEADS], tri,
                              dA.rearrange("p a b -> p (a b)"), start=True, stop=True)
                last.then_inc(dec_ps, 1)

            def xbc_(n, j):
                if j >= 2:
                    pe.wait_ge(conv_taken, nth(n, CB, j - 2))
                for k in range(KD):
                    last = mm(bank(4 + j % 2), win[:, k, INNER + j * P:INNER + (j + 1) * P], hT[:, k, :],
                              start=(k == 0), stop=(k == KD - 1))
                last.then_inc(xbc_ps, 1)

            def z_(b, t):
                if t >= 2:
                    pe.wait_ge(z_taken, nth(b, CH, t - 2))
                elif t == 1:
                    pe.wait_ge(dec_taken, nth(b, 1, 0))
                for k in range(KD):
                    last = mm(bank(t % 2), hT[:, k, t * P:(t + 1) * P], win[:, k, 0:INNER],
                              start=(k == 0), stop=(k == KD - 1))
                last.then_inc(z_ps, 1)

            def front(b, c, prev):
                l = slice(c * P, (c + 1) * P)
                if c == 0:
                    pe.wait_ge(xc_ready, nth(b, CB, CB - 1))
                    if prev:
                        pe.wait_ge(gate_taken, b * JB)
                        pe.wait_ge(up_taken, b * JB)
                else:
                    pe.wait_ge(xs_taken, nth(b, CH, c - 1))
                for j in range(4):
                    last = transposed(bank(2)[:, j * P:(j + 1) * P], xc[:, j, l])
                last.then_inc(xs_ps, 1)
                if c > 0:
                    pe.wait_ge(bg_taken, nth(b, CH, c - 1))
                transposed(bank(3)[:, 0:P], xc[:, 4, l])
                mm(bank(3)[:, P:2 * P], xc[:, 4, l], xc[:, 5, l], start=True, stop=True).then_inc(bg_ps, 1)
                pe.wait_ge(mda_ready, nth(b, CH, c))
                if c > 0:
                    pe.wait_ge(seg_taken, nth(b, CH, c - 1))
                elif prev:
                    pe.wait_ge(down_taken, b * CH)
                for i in range(2):
                    last = mm(bank(4 + i), tri_after, mda[:, c % 2, i * 512:(i + 1) * 512], start=True, stop=True)
                last.then_inc(seg_ps, 1)

            def back(b, c, prev):
                l = slice(c * P, (c + 1) * P)
                if c == 0:
                    if prev:
                        pe.wait_ge(h2T0_taken, b)
                        pe.wait_ge(h2T1_taken, b)
                else:
                    pe.wait_ge(y_taken, nth(b, CH, c - 1))
                    pe.wait_ge(s_taken, nth(b, CH - 1, c - 1))
                    mm(bank(7), xc[:, 5, l], st, start=True, stop=True).then_inc(off_ps, 1)
                pe.wait_ge(em_ready, nth(b, CH, c))
                pe.wait_ge(xdt_ready, nth(b, CH, c))
                for hh in range(HEADS):
                    last = mm(bank(6)[:, hh * HD:(hh + 1) * HD], em[:, c % 2, hh * P:(hh + 1) * P],
                              xdt[:, c % 2, hh * HD:(hh + 1) * HD], start=True, stop=True)
                last.then_inc(y_ps, 1)
                if c < CH - 1:
                    pe.wait_ge(xdtd_ready, nth(b, CH - 1, c))
                    if c == 0 and not prev:
                        pe.wait_ge(z_taken, CH)
                    mm(bank(1), bg[:, c % 2, 0:P], xdtd[:, c % 2, :], start=True, stop=True).then_inc(s_ps, 1)

            def yT_(b, c):
                pe.wait_ge(y4_ready, nth(b, CH, c))
                if c > 0:
                    pe.wait_ge(o_taken, nth(b, CH, c - 1))
                for j in range(4):
                    last = transposed(bank(0)[:, j * P:(j + 1) * P], yb[:, c % 2, j * P:(j + 1) * P])
                last.then_inc(yT_ps, 1)

            def out_(b, c):
                pe.wait_ge(yT_taken, nth(b, CH, c))
                if isinstance(b, int) and b == 0 and c == 0:
                    pe.wait_ge(wout_scaled, 1)
                for k in range(4):
                    last = mm(bank(0)[:, 0:D], yTs[:, k, :], wout[:, k, :], start=(k == 0), stop=(k == 3))
                last.then_inc(o_ps, 1)

            def xnT_(n, t, b):
                if t == 0:
                    pe.wait_ge(xn_ready, nth(n, 1, 0))
                if t < CH - 1:
                    pe.wait_ge(xs_taken, nth(b, CH, t + 1))
                for k in range(KD):
                    last = transposed(bank(2)[:, k * P:(k + 1) * P], xn[:, t, k * P:(k + 1) * P])
                last.then_inc(xnT_ps, 1)

            def logits(n, t, b):
                pe.wait_ge(xnT_taken, nth(n, CH, t))
                if t < CH - 1:
                    pe.wait_ge(bg_taken, nth(b, CH, t + 1))
                for k in range(KD):
                    last = mm(bank(3)[:, D + t * E:D + (t + 1) * E], xnT[:, k, :], wr[:, k, :], start=(k == 0), stop=(k == KD - 1))
                if t == CH - 1:
                    last.then_inc(lg_ps, 1)

            def positions(n):
                pe.wait_ge(sel_ready, nth(n, 1, 0))
                s = sel.rearrange("p a b -> p (a b)")
                mm(bank(6)[:, 0:CH * E], tri_before, s, start=True, stop=True)
                mm(bank(6)[:, CH * E:2 * CH * E], ones, s, start=True, stop=True).then_inc(pos_ps, 1)

            def mlp_up(b, j, nxt):
                if isinstance(b, int) and b == 0 and j == 0:
                    pe.wait_ge(rest_in, 16 * 5)
                w = min(P, INTER - j * P)
                bk = 2 * (j % 2)
                if j == 0:
                    pe.wait_ge(h2T0_taken, nth(b, 1, 0))
                    pe.wait_ge(h2T1_taken, nth(b, 1, 0))
                    pe.wait_ge(o_taken, nth(b, CH, CH - 1))
                    if nxt:
                        pe.wait_ge(z_taken, nth(b + 1, CH, CH - 1))
                elif j >= 2:
                    pe.wait_ge(gate_taken, nth(b, JB, j - 2))
                for k in range(KD):
                    last = mm(bank(bk)[0:w, :], wgate[:, k, j * P:j * P + w], h2T[:, k, :], start=(k == 0), stop=(k == KD - 1))
                last.then_inc(gate_ps, 1)
                if j >= 2:
                    pe.wait_ge(up_taken, nth(b, JB, j - 2))
                for k in range(KD):
                    last = mm(bank(bk + 1)[0:w, :], wup[:, k, j * P:j * P + w], h2T[:, k, :], start=(k == 0), stop=(k == KD - 1))
                last.then_inc(up_ps, 1)

            def mlp_down(b, t):
                if t == 0:
                    pe.wait_ge(up_taken, nth(b, JB, JB - 2))
                if t >= 2:
                    pe.wait_ge(down_taken, nth(b, CH, t - 2))
                for j in range(JB):
                    w = min(P, INTER - j * P)
                    if t == 0 and j == JB - 1:
                        pe.wait_ge(up_taken, nth(b, JB, j))
                    last = mm(bank(4 + t % 2)[:, 0:D], hid[0:w, j, t * P:(t + 1) * P], wdown[0:w, j, :],
                              start=(j == 0), stop=(j == JB - 1))
                last.then_inc(down_ps, 1)

            pe.wait_ge(small_in, 32)
            hT_(0)
            pe.wait_ge(win_in, 16)
            dt_(0)
            xbc_(0, 0)
            xbc_(0, 1)
            pe.wait_ge(dt_taken, 1)
            dec_(0)
            for t in range(CH):
                xbc_(0, t + 2)
                z_(0, t)
            pe.wait_ge(conv_taken, CB)

            def body(b, prev, nxt):
                front(b, 0, prev)
                for c in range(CH):
                    if c + 1 < CH:
                        front(b, c + 1, prev)
                    if prev and c > 0:
                        xnT_(b - 1, c, b)
                    if c > 0:
                        yT_(b, c - 1)
                    back(b, c, prev)
                    if prev and c == 0:
                        xnT_(b - 1, c, b)
                    if c > 0:
                        out_(b, c - 1)
                    if prev:
                        logits(b - 1, c, b)
                if prev:
                    pe.wait_ge(lg_taken, b)
                if nxt:
                    pe.wait_ge(bg_taken, nth(b, CH, CH - 1))
                    hT_(b + 1)
                yT_(b, CH - 1)
                if nxt:
                    pe.wait_ge(s_taken, nth(b, CH - 1, CH - 2))
                    dt_(b + 1)
                    pe.wait_ge(seg_taken, nth(b, CH, CH - 1))
                    xbc_(b + 1, 0)
                out_(b, CH - 1)
                if nxt:
                    xbc_(b + 1, 1)
                    pe.wait_ge(dt_taken, nth(b, 1, 1))
                    dec_(b + 1)
                    pe.wait_ge(o_taken, nth(b, CH, CH - 1))
                    z_(b + 1, 0)
                    z_(b + 1, 1)
                    xbc_(b + 1, 2)
                    xbc_(b + 1, 3)
                    z_(b + 1, 2)
                    z_(b + 1, 3)
                pe.wait_ge(h2_ready, nth(b, 1, 0))
                pe.wait_ge(y_taken, nth(b, CH, CH - 1))
                for k in range(KD):
                    for t in range(CH):
                        last = transposed(bank(6 + k)[:, t * P:(t + 1) * P], h1[:, t, k * P:(k + 1) * P])
                    last.then_inc(h2T_ps, 1)
                if nxt:
                    xbc_(b + 1, 4)
                    xbc_(b + 1, 5)
                else:
                    pe.wait_ge(s_taken, nth(b, CH - 1, CH - 2))
                    pe.wait_ge(bg_taken, nth(b, CH, CH - 1))
                    pe.wait_ge(seg_taken, nth(b, CH, CH - 1))
                for j in range(JB):
                    mlp_up(b, j, nxt)
                    if prev and j == 3:
                        positions(b - 1)
                if nxt:
                    pe.wait_ge(conv_taken, nth(b + 1, CB, CB - 1))
                for t in range(CH):
                    mlp_down(b, t)

            over_seqs(pe, body)
            pe.wait_ge(gate_taken, SEQS * JB)
            pe.wait_ge(down_taken, SEQS * CH)
            pe.wait_ge(xn_ready, SEQS)
            for k in range(KD):
                for t in range(CH):
                    last = transposed(bank(2 + k)[:, t * P:(t + 1) * P], xn[:, t, k * P:(k + 1) * P])
                last.then_inc(xnT_ps, 1)
            pe.wait_ge(xnT_taken, (SEQS - 1) * CH + 1)
            pe.wait_ge(xnT1_taken, 1)
            for t in range(CH):
                for k in range(KD):
                    last = mm(bank(4)[:, t * E:(t + 1) * E], h2T[:, k, t * P:(t + 1) * P], wr[:, k, :],
                              start=(k == 0), stop=(k == KD - 1))
            last.then_inc(lg_ps, 1)
            pe.wait_ge(pos_taken, SEQS - 1)
            positions(SEQS - 1)

            pe.wait_ge(recg_in, 16)
            for i in range(2):
                last = transposed(bank(7)[:, i * TILES:(i + 1) * TILES],
                                  recg[0:TILES, :].rearrange("t (s two) -> t two s", two=2)[:, i, :], TILES)
            last.then_inc(recT_ps, 1)

            pe.wait_ge(erow_ready, 1)
            pe.wait_ge(ids_ready, 1)
            pe.wait_ge(early_in, 48 * EARLY)

            def xT_(i):
                pe.wait_ge(xg_in, 16 * (i + 1))
                for k in range(KD):
                    last = transposed(bank(6)[:, k * P:(k + 1) * P], xg[:, k * P:(k + 1) * P])
                last.then_inc(xT_ps, 1)

            def up(e, off, bk, done):
                for k in range(KD):
                    for n in range(2):
                        last = mm(bank(bk + n)[:, 0:HALF], xT[:, k, :], expert_cols(e, off + k * M + n * HALF, HALF),
                                  start=(k == 0), stop=(k == KD - 1))
                last.then_inc(done, 1)

            def hT_turn(i):
                pe.wait_ge(b_taken, i + 1)
                for j in range(MB):
                    last = transposed(bank(4, 2)[:, j * P:(j + 1) * P], ha[:, j, :])
                last.then_inc(eT_ps, 1)

            def down(i, first=False):
                e = pe.value_load(erow[0:1, bass.ds(i, 1)], min_val=0, max_val=E - 1)
                pe.wait_ge(eT0_taken, i + 1)
                pe.wait_ge(eT1_taken, i + 1)
                if not first:
                    pe.wait_ge(yd_taken, i)
                for j in range(MB):
                    last = mm(bank(7)[:, 0:D], hTs[:, j, :], expert_cols(e, 2 * KD * M + j * D, D),
                              start=(j == 0), stop=(j == MB - 1))
                last.then_inc(yd_ps, 1)

            def tile(i, prev, nxt, second=False):
                e = pe.value_load(erow[0:1, bass.ds(i, 1)], min_val=0, max_val=E - 1)
                pe.wait_ge(xT_taken, i + 1)
                if prev:
                    pe.wait_ge(a_taken, i)
                up(e, 0, 0, a_ps)
                if prev:
                    hT_turn(i - 1)
                up(e, KD * M, 2, b_ps)
                if nxt:
                    xT_(i + 1)
                if prev:
                    down(i - 1, second)

            xT_(0)
            tile(0, False, True)
            tile(1, True, True, True)
            with pe.Fori(EARLY, E) as i:
                pe.wait_ge(expert_in, 48 * (i - (EARLY - 1)))
                tile(i, True, True)
            with pe.Fori(E, TILES - 1) as i:
                tile(i, True, True)
            tile(TILES - 1, True, False)
            hT_turn(TILES - 1)
            down(TILES - 1)

        @block.scalar
        def _(act):
            A = nc.scalar.activation

            act.wait_ge(small_in, 32)
            A(aneg, vec[:, V_ALOG:V_ALOG + HEADS], ACT.Exp).then_inc(aneg_exp, 1)

            def hT0(n):
                act.wait_ge(hT_ps, nth(n, 2, 0))
                A(hT[:, 0, :], bank(2), ACT.Copy, scale=vec[:, V_N1:V_N1 + 1]).then_inc(hT0_taken, 1)

            def dt_e(n):
                act.wait_ge(dt_abs, nth(n, 1, 0))
                A(dtu, dta, ACT.Exp, scale=-1.0).then_inc(dt_exp, 1)

            def dec_e(n):
                act.wait_ge(dec_ps, nth(n, 1, 0))
                A(dec.rearrange("p a b c -> p (a b c)"), bank(1)[:, 0:3 * CH * HEADS], ACT.Exp).then_inc(dec_taken, 1)

            def tap(n, j):
                act.wait_ge(xbc_ps, nth(n, CB, j))
                w = V_CW + j * TAPS + TAPS - 1
                A(xc[:, j, :], bank(4 + j % 2), ACT.Identity, scale=vec[:, w:w + 1],
                  bias=vec[:, V_CB + j:V_CB + j + 1]).then_inc(tap_done, 1)

            def conv_silu(n, j):
                act.wait_ge(conv_taken, nth(n, CB, j))
                A(xc[:, j, :], xc[:, j, :], ACT.Silu).then_inc(xc_ready, 1)

            def front(b, c):
                act.wait_ge(xs_ps, nth(b, CH, c))
                if not (isinstance(b, int) and b == 0 and c == 0):
                    act.wait_ge(xdt_ready, b * CH + c)
                    act.wait_ge(xsd_ready, b * CH + c)
                A(xs, bank(2), ACT.Copy).then_inc(xs_taken, 1)
                act.wait_ge(bg_ps, nth(b, CH, c))
                A(bg[:, c % 2, :], bank(3)[:, 0:2 * P], ACT.Copy).then_inc(bg_taken, 1)
                act.wait_ge(seg_ps, nth(b, CH, c))
                A(em[:, c % 2, :], bank(4, 2), ACT.Exp).then_inc(seg_taken, 1)

            def x_D(b, c):
                act.wait_ge(xs_taken, nth(b, CH, c))
                if not (isinstance(b, int) and b == 0 and c < 2):
                    act.wait_ge(y_taken, b * CH + c - 1)
                for hh in range(HEADS):
                    q = slice(hh * HD, (hh + 1) * HD)
                    last = A(xsd[:, c % 2, q], xs[:, q], ACT.Copy, scale=vec[:, V_D + hh:V_D + hh + 1])
                last.then_inc(xsd_ready, 1)


            def z_silu(b, t):
                act.wait_ge(z_ps, nth(b, CH, t))
                A(sz[:, t, :], bank(t % 2), ACT.Silu).then_inc(z_taken, 1)

            def yT_copy(b, c):
                act.wait_ge(yT_ps, nth(b, CH, c))
                A(yTs.rearrange("p a b -> p (a b)"), bank(0), ACT.Copy).then_inc(yT_taken, 1)

            def xnT_copy(n, t):
                act.wait_ge(xnT_ps, nth(n, CH, t))
                A(xnT.rearrange("p k n -> p (k n)"), bank(2)[:, 0:D], ACT.Copy).then_inc(xnT_taken, 1)

            def logits_copy(n):
                act.wait_ge(lg_ps, nth(n, 1, 0))
                A(lg.rearrange("p a b -> p (a b)"), bank(3)[:, D:D + CH * E], ACT.Copy).then_inc(lg_taken, 1)

            def square_y(b, c):
                act.wait_ge(y4_ready, nth(b, CH, c))
                A(junk_y, yb[:, c % 2, :], ACT.Square, accum_out=ssy[:, c:c + 1]).then_inc(ssy_ready, 1)

            def square_h(b, c):
                act.wait_ge(o_taken, nth(b, CH, c))
                if not (isinstance(b, int) and b == 0 and c == 0):
                    act.wait_ge(ssh_ready, b * CH + c)
                A(junk_h, h1[:, c, :], ACT.Square, accum_out=ssh[:, c:c + 1]).then_inc(ssh_ready, 1)

            def route_exp(n):
                act.wait_ge(route_d, nth(n, 1, 0))
                A(re_, rd, ACT.Exp).then_inc(route_e, 1)

            hT0(0)
            dt_e(0)
            tap(0, 0)
            tap(0, 1)
            dec_e(0)
            for t in range(CH):
                tap(0, t + 2)
                z_silu(0, t)
                conv_silu(0, t)
            conv_silu(0, CB - 2)
            conv_silu(0, CB - 1)

            def body(b, prev, nxt):
                front(b, 0)
                x_D(b, 0)
                for c in range(CH):
                    if c + 1 < CH:
                        front(b, c + 1)
                    if prev:
                        xnT_copy(b - 1, c)
                    if c >= 1:
                        yT_copy(b, c - 1)
                        square_y(b, c - 1)
                    if c + 1 < CH:
                        x_D(b, c + 1)
                    if c >= 2:
                        square_h(b, c - 2)
                if prev:
                    logits_copy(b - 1)
                square_h(b, CH - 2)
                if nxt:
                    hT0(b + 1)
                yT_copy(b, CH - 1)
                if nxt:
                    dt_e(b + 1)
                if prev:
                    route_exp(b - 1)
                square_y(b, CH - 1)
                if nxt:
                    tap(b + 1, 0)
                    tap(b + 1, 1)
                square_h(b, CH - 1)
                if nxt:
                    dec_e(b + 1)
                    conv_silu(b + 1, 0)
                    z_silu(b + 1, 0)
                    z_silu(b + 1, 1)
                    tap(b + 1, 2)
                    conv_silu(b + 1, 1)
                    tap(b + 1, 3)
                    z_silu(b + 1, 2)
                    z_silu(b + 1, 3)
                act.wait_ge(h2T_ps, nth(b, 2, 0))
                A(h2T[:, 0, :], bank(6), ACT.Copy, scale=vec[:, V_N2:V_N2 + 1]).then_inc(h2T0_taken, 1)
                if nxt:
                    conv_silu(b + 1, 2)
                    tap(b + 1, 4)
                    conv_silu(b + 1, 3)
                    tap(b + 1, 5)
                for j in range(JB):
                    w = min(P, INTER - j * P)
                    if nxt and j < 2:
                        conv_silu(b + 1, 4 + j)
                    act.wait_ge(gate_ps, nth(b, JB, j))
                    if j >= 2:
                        act.wait_ge(up_taken, nth(b, JB, j - 2))
                    A(sg[0:w, j % 2, :], bank(2 * (j % 2))[0:w, :], ACT.Silu).then_inc(gate_taken, 1)

            over_seqs(act, body)
            act.wait_ge(xnT_ps, (SEQS - 1) * CH + 1)
            A(h2T[:, 0, :], bank(2), ACT.Copy).then_inc(xnT_taken, 1)
            route_exp(SEQS - 1)

            def xT_copy(i):
                act.wait_ge(xT_ps, i + 1)
                A(xT.rearrange("p k n -> p (k n)"), bank(6)[:, 0:D], ACT.Copy).then_inc(xT_taken, 1)

            def turn_tail(i):
                act.wait_ge(eT_ps, i + 1)
                A(hTs[:, 4:MB, :].rearrange("p a b -> p (a b)"), bank(5)[:, 0:(MB - 4) * P], ACT.Copy).then_inc(eT1_taken, 1)

            def tile(i, prev, nxt):
                act.wait_ge(a_ps, i + 1)
                if prev:
                    act.wait_ge(b_taken, i)
                A(sa, bank(0, 2).rearrange("p (a b) -> p a b", a=2)[:, :, 0:HALF], ACT.Silu).then_inc(a_taken, 1)
                if prev:
                    turn_tail(i - 1)
                if nxt:
                    xT_copy(i + 1)

            xT_copy(0)
            tile(0, False, True)
            with act.Fori(1, TILES - 1) as i:
                tile(i, True, True)
            tile(TILES - 1, True, False)
            turn_tail(TILES - 1)

        @block.vector
        def _(v):
            V = nc.vector
            idle = cols(8)

            def pass_wait(k):
                V.memset(idle[:, k:k + 1], 0.0)

            ln1 = Steps(v, ln1_step, 2)
            dts_ = Steps(v, dt_step, 6 + SERIES)
            conv = Steps(v, conv_step, TAPS - 2)
            rt_ = Steps(v, route_step, 25)
            tab = Steps(v, table_step, 11)

            def ln1_stats(n):
                if isinstance(n, int) and n == 0:
                    v.wait_ge(x_first, 16)
                ln1.start(n)
                for t in range(CH):
                    last = V.bn_stats(st6[:, t, :], x[:, bass.ds(n * CH + t, 1), :].rearrange("p a d -> p (a d)"))
                ln1.then(last)
                pass_wait(0)
                for t in range(CH):
                    last = V.bn_aggr(mv[:, t, :], st6[:, t, :])
                ln1.then(last)
                ln1.end()
                V.tensor_scalar_add(ve, mv[:, :, 1], LN_EPS).then_inc(ln1_var, 1)

            def ln1_h(n):
                v.wait_ge(ln1_r, nth(n, 1, 0))
                for t in range(CH):
                    last = V.tensor_scalar(h[:, t, :], x[:, bass.ds(n * CH + t, 1), :].rearrange("p a d -> p (a d)"),
                                           mv[:, t, 0:1], rr[:, t:t + 1], ALU.subtract, ALU.mult)
                last.then_inc(h_ready, 1)

            def hT1(n):
                v.wait_ge(hT_ps, nth(n, 2, 1))
                V.tensor_scalar(hT[:, 1, :], bank(3), vec[:, V_N1 + 1:V_N1 + 2], None, ALU.mult).then_inc(hT1_taken, 1)

            def dt_abs_(n):
                v.wait_ge(dt_ps, nth(n, 1, 0))
                V.tensor_tensor(dtx, bank(1)[:, 0:CH * HEADS].rearrange("p (a b) -> p a b", b=HEADS),
                                vec[:, V_DTB:V_DTB + HEADS].unsqueeze(1).to_broadcast([P, CH, HEADS]), ALU.add).then_inc(dt_taken, 1)
                v.wait_ge(dt_taken, nth(n, 1, 0))
                V.scalar_tensor_tensor(dta, dtx, -1.0, dtx, ALU.mult, ALU.max).then_inc(dt_abs, 1)

            def dt_softplus(n):
                dts_.start(n)
                v.wait_ge(dt_exp, nth(n, 1, 0))
                dts_.then(V.tensor_scalar_add(dtd, dtu, 2.0))
                dts_.then(V.reciprocal(dtr, dtd))
                dts_.then(V.tensor_tensor(dts, dtu, dtr, ALU.mult))
                dts_.then(V.tensor_tensor(dts2, dts, dts, ALU.mult))
                last = V.tensor_scalar(dtq, dts2, 1.0 / (2 * SERIES + 1), None, ALU.mult)
                for k in range(SERIES - 1, 0, -1):
                    dts_.then(last)
                    last = V.scalar_tensor_tensor(dtq, dtq, 1.0 / (2 * k + 1), dts2, ALU.add, ALU.mult)
                dts_.then(last)
                V.tensor_scalar(dtl, dtx, 0.0, None, ALU.max)
                dts_.then(V.scalar_tensor_tensor(dtp, dtq, 1.0, dts, ALU.add, ALU.mult))
                dts_.then(V.scalar_tensor_tensor(dtv, dtp, 2.0, dtl, ALU.mult, ALU.add))
                dts_.end()
                V.tensor_tensor(dA, dtv, aneg.unsqueeze(1).to_broadcast([P, CH, HEADS]), ALU.mult).then_inc(dA_ready, 1)

            def conv_taps(n, j):
                conv.start(n * CB + j)
                v.wait_ge(tap_done, nth(n, CB, j))
                for s in range(1, TAPS):
                    w = V_CW + j * TAPS + TAPS - 1 - s
                    last = V.scalar_tensor_tensor(xc[:, j, s:SEQ], bank(4 + j % 2)[:, 0:SEQ - s], vec[:, w:w + 1],
                                                  xc[:, j, s:SEQ], ALU.mult, ALU.add)
                    if s < TAPS - 1:
                        conv.then(last)
                conv.end()
                last.then_inc(conv_taken, 1)

            def heads(a):
                return a.rearrange("p (h q) -> p h q", h=HEADS)

            def over_head(a, n=HD):
                return a.unsqueeze(2).to_broadcast([P, HEADS, n])

            def front(b, c):
                v.wait_ge(bg_taken, nth(b, CH, c))
                V.tensor_tensor(gm[:, c % 2, :], bg[:, c % 2, P:2 * P], tri_upto, ALU.mult).then_inc(gm_step, 1)
                v.wait_ge(gm_step, nth(b, CH, c))
                v.wait_ge(seg_taken, nth(b, CH, c))
                V.tensor_tensor(heads(em[:, c % 2, :]), heads(em[:, c % 2, :]),
                                gm[:, c % 2, :].unsqueeze(1).to_broadcast([P, HEADS, P]), ALU.mult).then_inc(em_ready, 1)

            def off(b, c):
                v.wait_ge(off_ps, nth(b, CH - 1, c - 1))
                V.tensor_tensor(heads(yb[:, c % 2, :]), heads(bank(7)), over_head(dec[:, 1, c, :]), ALU.mult).then_inc(off_scaled, 1)
                if c < CH - 1:
                    V.tensor_tensor(heads(st), heads(st), over_head(dec[:, 2, c, :]), ALU.mult).then_inc(s_step, 1)

            def y_(b, c):
                v.wait_ge(y_ps, nth(b, CH, c))
                if c == 0:
                    v.wait_ge(xsd_ready, nth(b, CH, c))
                    V.tensor_tensor(yb[:, 0, :], xsd[:, 0, :], bank(6), ALU.add).then_inc(y_taken, 1)
                else:
                    v.wait_ge(y3_ready, nth(b, CH - 1, c - 1))
                    V.tensor_tensor(yb[:, c % 2, :], yb[:, c % 2, :], bank(6), ALU.add).then_inc(y_taken, 1)

            def state(b, c):
                if c == 0:
                    v.wait_ge(s_ps, nth(b, CH - 1, c))
                    V.tensor_copy(st, bank(1)).then_inc(s_taken, 1)
                elif c < CH - 1:
                    v.wait_ge(s_step, nth(b, CH - 2, c - 1))
                    v.wait_ge(s_ps, nth(b, CH - 1, c))
                    V.tensor_tensor(st, st, bank(1), ALU.add).then_inc(s_taken, 1)

            def decayed_x(b, c):
                v.wait_ge(xdt_ready, nth(b, CH, c))
                if c == 0:
                    v.wait_ge(dec_taken, nth(b, 1, 0))
                V.tensor_tensor(heads(xdtd[:, c % 2, :]), heads(xdt[:, c % 2, :]), over_head(dec[:, 0, c, :]), ALU.mult).then_inc(xdtd_ready, 1)

            def h1_(b, c):
                V.tensor_scalar(ab, x[:, bass.ds(b * CH + c, 1), :].rearrange("p a d -> p (a d)"),
                                cur_mv[:, c, 0:1], cur_rs[:, c:c + 1], ALU.subtract, ALU.mult).then_inc(a_step, 1)
                v.wait_ge(a_step, nth(b, CH, c))
                v.wait_ge(o_ps, nth(b, CH, c))
                v.wait_ge(ry_ready, nth(b, CH, c))
                V.scalar_tensor_tensor(h1[:, c, :], bank(0)[:, 0:D], ry[:, c:c + 1], ab, ALU.mult, ALU.add).then_inc(o_taken, 1)
                v.wait_ge(o_taken, nth(b, CH, c))
                xt = x[:, bass.ds(b * CH + c, 1), :].rearrange("p a d -> p (a d)")
                V.tensor_tensor(xt, xt, h1[:, c, :], ALU.add).then_inc(xh_ready, 1)

            def xn_(n):
                v.wait_ge(ln2_r, nth(n, 1, 0))
                if not (isinstance(n, int) and n == 0):
                    v.wait_ge(xn_out, 16 * n)
                for t in range(CH):
                    last = V.tensor_scalar(xn[:, t, :], x[:, bass.ds(n * CH + t, 1), :].rearrange("p a d -> p (a d)"),
                                           mv2[:, t, 0:1], rs2[:, t:t + 1], ALU.subtract, ALU.mult)
                last.then_inc(xn_ready, 1)

            def over_e(a):
                return a.unsqueeze(2).to_broadcast([P, CH, E])

            def over_t(a):
                return a.unsqueeze(1).to_broadcast([P, CH, E])

            def route_max(n):
                rt_.start(n)
                v.wait_ge(lg_taken, nth(n, 1, 0))
                rt_.then(V.tensor_reduce(rmx, lg, AX, ALU.max))
                V.tensor_tensor(rd, lg, over_e(rmx), ALU.subtract).then_inc(route_d, 1)

            def pick(p, most, o, m):
                rt_.then(V.tensor_reduce(most, p, AX, ALU.max))
                rt_.then(V.tensor_tensor(req, p, over_e(most), ALU.is_equal))
                rt_.then(V.tensor_tensor(rsc, req, over_t(cst[:, C_RANK:C_RANK + E]), ALU.mult))
                rt_.then(V.tensor_reduce(m, rsc, AX, ALU.max))
                rt_.then(V.tensor_tensor(o, rsc, over_e(m), ALU.is_equal))

            def route_pick(n):
                v.wait_ge(route_e, nth(n, 1, 0))
                rt_.then(V.tensor_reduce(rsum, re_, AX, ALU.add))
                rt_.then(V.reciprocal(rrec, rsum))
                rt_.then(V.tensor_tensor(rp, re_, over_e(rrec), ALU.mult))
                pick(rp, p1, o1, rm1)
                rt_.then(V.scalar_tensor_tensor(rq, o1, -2.0, rp, ALU.mult, ALU.add))
                pick(rq, p2, o2, rm2)
                V.tensor_tensor(sel, o1, o2, ALU.add).then_inc(sel_ready, 1)
                rt_.then(V.tensor_tensor(ps12, p1, p2, ALU.add))
                rt_.then(V.reciprocal(pr12, ps12))
                if not (isinstance(n, int) and n == 0):
                    v.wait_ge(rec_out, 16 * CH * TOP * n)
                for k, p in enumerate((p1, p2)):
                    V.tensor_tensor(rec[:, :, k, 1], p, pr12, ALU.mult)
                    V.tensor_copy(rec[:, :, k, 0], cst[:, bass.ds(C_TOKEN + n * CH, CH)])

            def route_slots(n):
                v.wait_ge(pos_ps, nth(n, 1, 0))
                for t in range(CH):
                    V.tensor_tensor(rpos[:, t, :], bank(6)[:, t * E:(t + 1) * E], run, ALU.add)
                    last = V.tensor_tensor(run, run, bank(6)[:, (CH + t) * E:(CH + t + 1) * E], ALU.add)
                    if t < CH - 1:
                        rt_.then(last)
                last.then_inc(pos_taken, 1)
                v.wait_ge(pos_taken, nth(n, 1, 0))
                rt_.then(V.tensor_tensor(radr, rpos, over_t(cst[:, C_LISTS:C_LISTS + E]), ALU.add))
                for k, o in enumerate((o1, o2)):
                    rt_.then(V.tensor_tensor(rt, o, radr, ALU.mult))
                    rt_.then(V.tensor_reduce(slotf[:, :, k], rt, AX, ALU.add))
                V.tensor_copy(slot, slotf).then_inc(rec_ready, 1)
                rt_.end()

            V.memset(zero, 0.0).then_inc(zeroed, 1)
            V.memset(run, 0.0).then_inc(run_zero, 1)
            v.wait_ge(run_zero, 1)
            v.wait_ge(aneg_exp, 1)
            V.tensor_scalar(aneg, aneg, -1.0, None, ALU.mult).then_inc(aneg_ready, 1)
            v.wait_ge(aneg_ready, 1)
            ln1_stats(0)
            ln1_h(0)
            hT1(0)
            dt_abs_(0)
            dt_softplus(0)
            for j in range(CB):
                conv_taps(0, j)
            v.wait_ge(x_rest, 16)

            def body(b, prev, nxt):
                V.tensor_copy(cur_mv, mv)
                V.tensor_copy(cur_rs, rs).then_inc(cur_kept, 1)
                v.wait_ge(cur_kept, nth(b, 1, 0))
                if prev:
                    xn_(b - 1)
                front(b, 0)
                decayed_x(b, 0)
                for c in range(CH):
                    if c + 1 < CH:
                        front(b, c + 1)
                    if c >= 2:
                        v.wait_ge(yT_taken, nth(b, CH, c - 2))
                    if c > 0:
                        off(b, c)
                    y_(b, c)
                    state(b, c)
                    if c > 0:
                        h1_(b, c - 1)
                    if c + 1 < CH - 1:
                        decayed_x(b, c + 1)
                    if nxt and c == 0:
                        ln1_stats(b + 1)
                    if nxt and c == 2:
                        ln1_h(b + 1)
                if nxt:
                    hT1(b + 1)
                if prev:
                    route_max(b - 1)
                if nxt:
                    dt_abs_(b + 1)
                    dt_softplus(b + 1)
                h1_(b, CH - 1)
                if nxt:
                    conv_taps(b + 1, 0)
                    conv_taps(b + 1, 1)
                v.wait_ge(rh_ready, nth(b, 1, 0))
                v.wait_ge(xh_ready, nth(b, CH, CH - 1))
                for t in range(CH):
                    last = V.tensor_scalar(h1[:, t, :], h1[:, t, :], rh[:, t:t + 1], None, ALU.mult)
                last.then_inc(h2_ready, 1)
                if nxt:
                    conv_taps(b + 1, 2)
                    conv_taps(b + 1, 3)
                v.wait_ge(h2T_ps, nth(b, 2, 1))
                V.tensor_scalar(h2T[:, 1, :], bank(7), vec[:, V_N2 + 1:V_N2 + 2], None, ALU.mult).then_inc(h2T1_taken, 1)
                if nxt:
                    conv_taps(b + 1, 4)
                    conv_taps(b + 1, 5)
                for j in range(JB):
                    w = min(P, INTER - j * P)
                    v.wait_ge(up_ps, nth(b, JB, j))
                    v.wait_ge(gate_taken, nth(b, JB, j))
                    V.tensor_tensor(hid[0:w, j, :], sg[0:w, j % 2, :], bank(2 * (j % 2) + 1)[0:w, :], ALU.mult).then_inc(up_taken, 1)
                    if prev and j == 1:
                        route_pick(b - 1)
                if prev:
                    route_slots(b - 1)
                for t in range(CH):
                    xt = x[:, bass.ds(b * CH + t, 1), :].rearrange("p a d -> p (a d)")
                    v.wait_ge(down_ps, nth(b, CH, t))
                    V.tensor_tensor(xt, xt, bank(4 + t % 2)[:, 0:D], ALU.add).then_inc(down_taken, 1)
                    v.wait_ge(down_taken, nth(b, CH, t))
                    pass_wait(1)
                    V.bn_stats(st6b[:, t, :], xt).then_inc(ln2_step, 1)
                v.wait_ge(ln2_step, nth(b, CH + 1, CH - 1))
                pass_wait(2)
                for t in range(CH):
                    last = V.bn_aggr(mv2[:, t, :], st6b[:, t, :])
                last.then_inc(ln2_step, 1)
                v.wait_ge(ln2_step, nth(b, CH + 1, CH))
                V.tensor_scalar_add(ve2, mv2[:, :, 1], LN_EPS).then_inc(ln2_var, 1)

            over_seqs(v, body)
            xn_(SEQS - 1)
            v.wait_ge(xnT_ps, (SEQS - 1) * CH + 2)
            V.tensor_copy(h2T[:, 1, :], bank(3)).then_inc(xnT1_taken, 1)
            v.wait_ge(lg_ps, SEQS)
            V.tensor_copy(lg.rearrange("p a b -> p (a b)"), bank(4)[:, 0:CH * E]).then_inc(lg_taken, 1)
            route_max(SEQS - 1)
            route_pick(SEQS - 1)
            route_slots(SEQS - 1)

            tab.start(0)
            tab.then(V.tensor_tensor(full, run.unsqueeze(2).to_broadcast([P, E, LIST]),
                                     cst[:, C_FULL:C_FULL + LIST].unsqueeze(1).to_broadcast([P, E, LIST]), ALU.is_gt))
            tab.then(V.tensor_reduce(nt, full, AX, ALU.add))
            tab.then(V.tensor_scalar(nt, nt, 1.0, None, ALU.max))
            tab.then(V.tensor_tensor_scan(upto, ones[:, 0:E], nt, 0.0, ALU.mult, ALU.add))
            tab.then(V.tensor_scalar(ge[:, 0:E - 1], upto[:, 0:E - 1], cst[:, C_ROW:C_ROW + 1], None, ALU.is_le))
            tab.then(V.tensor_tensor(gn[:, 0:E - 1], ge[:, 0:E - 1], nt[:, 0:E - 1], ALU.mult))
            tab.then(V.tensor_reduce(scol, gn[:, 0:E - 1], AX, ALU.add))
            tab.then(V.tensor_reduce(ecol, ge[:, 0:E - 1], AX, ALU.add))
            tab.then(V.tensor_scalar(rcol, ecol, float(LIST), cst[:, C_ROW:C_ROW + 1], ALU.mult, ALU.add))
            V.tensor_tensor(ridx, rcol, scol, ALU.subtract).then_inc(ridx_ready, 1)
            tab.then(V.tensor_tensor(ge_row[0:1, :, 0:E - 1],
                                     upto[0:1, 0:E - 1].unsqueeze(1).to_broadcast([1, TILES, E - 1]),
                                     cst[0:1, C_TILE:C_TILE + TILES].unsqueeze(2).to_broadcast([1, TILES, E - 1]), ALU.is_le))
            tab.then(V.tensor_reduce(erowf[0:1, :], ge_row[0:1, :, 0:E - 1], AX, ALU.add))
            tab.end()
            V.tensor_copy(erow[0:1, :], erowf[0:1, :]).then_inc(erow_ready, 1)
            v.wait_ge(recT_ps, 1)
            V.tensor_copy(ids, bank(7)[:, 0:TILES])
            V.tensor_copy(wts, bank(7)[:, TILES:2 * TILES]).then_inc(ids_ready, 1)
            v.wait_ge(ids_ready, 1)

            def turn_head(i):
                v.wait_ge(eT_ps, i + 1)
                V.tensor_copy(hTs[:, 0:4, :].rearrange("p a b -> p (a b)"), bank(4)).then_inc(eT0_taken, 1)

            def weigh(i, first=False):
                v.wait_ge(yd_ps, i + 1)
                if not first:
                    v.wait_ge(y_added, 16 * i)
                V.tensor_scalar(ys, bank(7)[:, 0:D], wts[:, bass.ds(i, 1)], None, ALU.mult).then_inc(yd_taken, 1)

            def tile(i, prev, second=False):
                if prev:
                    turn_head(i - 1)
                v.wait_ge(b_ps, i + 1)
                v.wait_ge(a_taken, i + 1)
                V.tensor_tensor(ha.rearrange("p a b -> p (a b)").rearrange("p (a b) -> p a b", a=2), sa,
                                bank(2, 2).rearrange("p (a b) -> p a b", a=2)[:, :, 0:HALF], ALU.mult).then_inc(b_taken, 1)
                if prev:
                    weigh(i - 1, second)

            tile(0, False)
            tile(1, True, True)
            with v.Fori(2, TILES) as i:
                tile(i, True)
            turn_head(TILES - 1)
            weigh(TILES - 1)

        @block.gpsimd
        def _(g):
            G = nc.gpsimd
            idle = cols(8)

            def pass_wait(k):
                G.tensor_tensor(idle[:, k:k + 1], half[:, 0:1], half[:, 0:1], ALU.add)

            half = cst[:, C_POW:C_POW + 4]
            g_ln1 = Steps(g, pool_ln1, 4)

            def heads(a):
                return a.rearrange("p (h q) -> p h q", h=HEADS)

            def over_head(a, n=HD):
                return a.unsqueeze(2).to_broadcast([P, HEADS, n])

            def ln1_scale(n):
                g.wait_ge(ln1_var, nth(n, 1, 0))
                g_ln1.start(n)
                g_ln1.then(G.tensor_tensor(rs, ve, half, ALU.pow))
                g_ln1.then(G.tensor_tensor(t4a, rs, rs, ALU.mult))
                g_ln1.then(G.tensor_tensor(t4b, t4a, mv[:, :, 1], ALU.mult))
                pass_wait(0)

            def rms_scale(n):
                G.tensor_scalar(t4a, t4b, 1.0, RMS_EPS, ALU.mult, ALU.add).then_inc(pool_rh, 1)
                g.wait_ge(pool_rh, nth(n, 1, 0))
                g_ln1.then(G.tensor_tensor(t4b, t4a, half, ALU.pow))
                g_ln1.end()
                G.tensor_tensor(rr, rs, t4b, ALU.mult).then_inc(ln1_r, 1)

            def masked_dA(n, c):
                g.wait_ge(dA_ready, nth(n, 1, 0))
                if not (isinstance(n, int) and n == 0 and c < 2):
                    g.wait_ge(seg_ps, n * CH + c - 1)
                G.tensor_tensor(heads(mda[:, c % 2, :]), tri_upto.unsqueeze(1).to_broadcast([P, HEADS, P]),
                                over_head(dA[:, c, :], P), ALU.mult).then_inc(mda_ready, 1)

            def scaled_x(b, c):
                g.wait_ge(xs_taken, nth(b, CH, c))
                G.tensor_tensor(heads(xdt[:, c % 2, :]), heads(xs), over_head(dtv[:, c, :]), ALU.mult).then_inc(xdt_ready, 1)

            def plus_x_D(b, c):
                g.wait_ge(xsd_ready, nth(b, CH, c))
                g.wait_ge(off_scaled, nth(b, CH - 1, c - 1))
                G.tensor_tensor(yb[:, c % 2, :], yb[:, c % 2, :], xsd[:, c % 2, :], ALU.add).then_inc(y3_ready, 1)

            def gated(b, c):
                g.wait_ge(y_taken, nth(b, CH, c))
                if c == 0:
                    g.wait_ge(z_taken, nth(b, CH, CH - 1))
                G.tensor_tensor(yb[:, c % 2, :], yb[:, c % 2, :], sz[:, c, :], ALU.mult).then_inc(y4_ready, 1)

            def scale_y(b, c):
                g.wait_ge(ssy_ready, nth(b, CH, c))
                pass_wait(1)
                G.tensor_scalar(vy[:, c:c + 1], ssy[:, c:c + 1], 1.0 / INNER, RMS_EPS, ALU.mult, ALU.add).then_inc(pool_ry, 1)
                g.wait_ge(pool_ry, nth(b, CH + 1, c))
                G.tensor_tensor(ry[:, c:c + 1], vy[:, c:c + 1], half[:, 0:1], ALU.pow).then_inc(ry_ready, 1)

            def scatter(n):
                g.wait_ge(lists_in, 16)
                g.wait_ge(rec_ready, nth(n, 1, 0))
                pass_wait(2)
                for t in range(CH):
                    for k in range(TOP):
                        G.indirect_dma_start(lists, bass.IndirectOffsetOnAxis(ap=slot[:, t, k:k + 1], axis=0),
                                             rec[:, t, k, :], None).then_inc(rec_out, 16)

            ln1_scale(0)
            rms_scale(0)
            g.wait_ge(wout_in, 16)
            for k in range(4):
                last = G.tensor_tensor(wout[:, k, :], wout[:, k, :], vec[:, V_MN + k:V_MN + k + 1].to_broadcast([P, D]), ALU.mult)
            last.then_inc(wout_scaled, 1)
            masked_dA(0, 0)
            masked_dA(0, 1)

            def body(b, prev, nxt):
                scaled_x(b, 0)
                for c in range(CH):
                    if c + 2 < CH:
                        masked_dA(b, c + 2)
                    if c + 1 < CH:
                        scaled_x(b, c + 1)
                    if c > 0:
                        plus_x_D(b, c)
                        scale_y(b, c - 1)
                    gated(b, c)
                    if nxt and c == 1:
                        ln1_scale(b + 1)
                    if nxt and c == 2:
                        rms_scale(b + 1)
                scale_y(b, CH - 1)
                g.wait_ge(ssh_ready, nth(b, CH, CH - 1))
                pass_wait(3)
                G.tensor_scalar(vh, ssh, 1.0 / D, RMS_EPS, ALU.mult, ALU.add).then_inc(pool_ry, 1)
                g.wait_ge(pool_ry, nth(b, CH + 1, CH))
                G.tensor_tensor(rh, vh, half, ALU.pow).then_inc(rh_ready, 1)
                if nxt:
                    masked_dA(b + 1, 0)
                    masked_dA(b + 1, 1)
                if prev:
                    scatter(b - 1)
                g.wait_ge(ln2_var, nth(b, 1, 0))
                G.tensor_tensor(rs2, ve2, half, ALU.pow).then_inc(ln2_r, 1)

            over_seqs(g, body)
            scatter(SEQS - 1)
            g.wait_ge(rec_out, 16 * CH * TOP * SEQS)
            g.wait_ge(ridx_ready, 1)
            G.indirect_dma_start(recg[0:TILES, :], None, lists.rearrange("(t s) two -> t (s two)", s=P),
                                 bass.IndirectOffsetOnAxis(ap=ridx[0:TILES, :], axis=0)).then_inc(recg_in, 16)

            g.wait_ge(ids_ready, 1)
            g.wait_ge(xn_out, 16 * SEQS)
            g.wait_ge(x1_out, 16 * SEQS)
            g.wait_ge(pads_out, 32)

            def gather(i):
                G.tensor_copy(gidx, ids[:, bass.ds(i, 1)]).then_inc(gidx_ready, 1)
                g.wait_ge(gidx_ready, i + 1)
                pass_wait(4)
                G.indirect_dma_start(xg, None, xn_rows, bass.IndirectOffsetOnAxis(ap=gidx, axis=0)).then_inc(xg_in, 16)

            def add_rows(i, first=False):
                g.wait_ge(yd_taken, i + 1)
                if not first:
                    g.wait_ge(y_added, 16 * i)
                    pass_wait(5)
                G.tensor_copy(sidx, ids[:, bass.ds(i, 1)]).then_inc(sidx_ready, 1)
                g.wait_ge(sidx_ready, i + 1)
                pass_wait(6)
                G.indirect_dma_start(out, bass.IndirectOffsetOnAxis(ap=sidx, axis=0), ys, None,
                                     compute_op=ALU.add, bounds_check=TOKENS + P - 1, oob_is_err=True).then_inc(y_added, 16)

            gather(0)
            g.wait_ge(xT_ps, 1)
            gather(1)
            g.wait_ge(xT_ps, 2)
            gather(2)
            add_rows(0, True)
            with g.Fori(1, TILES - 2) as i:
                g.wait_ge(xT_ps, i + 2)
                pass_wait(7)
                gather(i + 2)
                add_rows(i)
            add_rows(TILES - 2)
            add_rows(TILES - 1)
            g.wait_ge(y_added, 16 * TILES)


_VECTORS = ("L0_attn_norm1_w", "L0_attn_mixer_norm_w", "L0_attn_norm2_w")


def kernel(**inputs):
    import concourse.bacc as bacc
    from concourse.bass_utils import run_bass_kernel_spmd

    a = {k: np.asarray(v) for k, v in inputs.items()}

    def down_partitions(v):
        return v.reshape(-1, P).T

    def all_partitions(v):
        return np.broadcast_to(v[None, :], (P, v.shape[0]))

    conv_w = a["L0_attn_conv_w"].reshape(CB, P, TAPS).transpose(1, 0, 2).reshape(P, CB * TAPS)
    vecs = np.concatenate(
        [down_partitions(a[n]) for n in _VECTORS]
        + [conv_w, down_partitions(a["L0_attn_conv_b"])]
        + [all_partitions(a[n]) for n in ("L0_attn_dt_bias", "L0_attn_A_log", "L0_attn_D_param")], axis=1)
    consts, empty = constants()
    arrays = {
        "hidden": a["L0_attn_hidden_states"].reshape(TOKENS, D), "vecs": vecs, "consts": consts, "empty": empty,
        "in_proj": a["L0_attn_in_proj_w"], "out_proj": a["L0_attn_out_proj_w"], "gate": a["L0_attn_gate_w"],
        "up": a["L0_attn_up_w"], "down": a["L0_attn_down_w"], "router": a["L0_ffn_gate_w"],
        "w1": a["L0_ffn_w1"], "w2": a["L0_ffn_w2"], "w3": a["L0_ffn_w3"],
    }
    arrays = {f"in_{k}": np.ascontiguousarray(v) for k, v in arrays.items()}
    nc = bacc.Bacc("TRN2", target_bir_lowering=False, num_devices=1)
    args = [nc.dram_tensor(k, v.shape, mybir.dt.from_np(v.dtype), kind="ExternalInput").ap() for k, v in arrays.items()]
    out = nc.dram_tensor("out_rows", (TOKENS + P, D), F32, kind="ExternalOutput").ap()
    build(nc, *args, out)
    r = run_bass_kernel_spmd(nc, [arrays], core_ids=[0])
    return np.asarray(r.results[0]["out_rows"])[:TOKENS].reshape(SEQS, SEQ, D)
```

```python
from contextlib import ExitStack

import numpy as np

import concourse.bass as bass
from concourse import mybir

P = 128
SEQS, SEQ = 4, 512
TOKENS = SEQS * SEQ
CH = SEQ // P
D = 256
KD = D // P
INNER = 512
HEADS, HD = 8, 64
STATE = 128
CONV = INNER + 2 * STATE
CB = CONV // P
TAPS = 4
PROJ = 2 * INNER + 2 * STATE + HEADS
INTER = 704
JB = -(-INTER // P)
REST = INTER - (JB - 1) * P
assert 2 * REST == P
E, TOP = 8, 2
M = 896
MB = M // P
HALF = M // 2
TILES = TOKENS * TOP // P + E - 1
LIST = TOKENS // P
SLOT_TILES = E * LIST + TILES - E - LIST + 1
EXPERT = 2 * KD * M + MB * D
EARLY = 2
LN_EPS, RMS_EPS = 1e-5, 1e-6
SERIES = 8

F32 = mybir.dt.float32
I32 = mybir.dt.int32
ALU = mybir.AluOpType
ACT = mybir.ActivationFunctionType
AX = mybir.AxisListType.X

C_ID, C_UPTO, C_AFTER, C_BEFORE, C_ONES = 0, P, 2 * P, 3 * P, 4 * P
C_RANK = 5 * P
C_LISTS = C_RANK + E
C_FULL = C_LISTS + E
C_TILE = C_FULL + LIST
C_ROW = C_TILE + TILES
C_TOKEN = C_ROW + 1
C_POW = C_TOKEN + SEQS * CH
N_CONST = C_POW + 4
V_N1, V_MN, V_N2 = 0, KD, KD + 4
V_CW = V_N2 + KD
V_CB = V_CW + CB * TAPS
V_DTB = V_CB + CB
V_ALOG = V_DTB + HEADS
V_D = V_ALOG + HEADS
N_VEC = V_D + HEADS


def constants():
    c = np.zeros((P, N_CONST), np.float32)
    r = np.arange(P)
    c[:, C_ID:C_ID + P] = np.eye(P)
    c[:, C_UPTO:C_UPTO + P] = r[:, None] <= r[None, :]
    c[:, C_AFTER:C_AFTER + P] = r[:, None] > r[None, :]
    c[:, C_BEFORE:C_BEFORE + P] = r[:, None] < r[None, :]
    c[:, C_ONES:C_ONES + P] = 1.0
    c[:, C_RANK:C_RANK + E] = E - np.arange(E)
    c[:, C_LISTS:C_LISTS + E] = TOKENS * np.arange(E)
    c[:, C_FULL:C_FULL + LIST] = P * np.arange(LIST)
    c[:, C_TILE:C_TILE + TILES] = np.arange(TILES)
    c[:, C_ROW] = r
    c[:, C_TOKEN:C_TOKEN + SEQS * CH] = r[:, None] + P * np.arange(SEQS * CH)
    c[:, C_POW:C_POW + 4] = -0.5
    empty = np.zeros((SLOT_TILES, P, 2), np.float32)
    empty[:, :, 0] = TOKENS + r
    return c, empty.reshape(SLOT_TILES * P, 2)


class Steps:

    def __init__(self, eng, sem, length):
        self.eng, self.sem, self.length = eng, sem, length

    def start(self, n):
        self.n, self.k = n, 0

    def then(self, ins):
        self.k += 1
        assert self.k <= self.length
        ins.then_inc(self.sem, 1)
        self.eng.wait_ge(self.sem, self.n * self.length + self.k)

    def end(self):
        assert self.k == self.length, (self.k, self.length)


def nth(n, per, k):
    return n * per + (k + 1)


def build(nc, hidden, vecs, consts, empty, in_proj, out_proj, gate_w, up_w, down_w,
          router_w, w1, w2, w3, out):
    xn_rows = nc.dram_tensor("xn_rows", [TOKENS + P, D], F32).ap()
    lists = nc.dram_tensor("lists", [SLOT_TILES * P, 2], F32).ap()

    ctx = ExitStack()
    with ctx:
        def sem(name):
            return ctx.enter_context(nc.semaphore(name))

        COLS = 53200
        big = ctx.enter_context(nc.sbuf_tensor("big", [P, COLS], F32))
        at = [EARLY * EXPERT]

        def cols(*shape):
            n = int(np.prod(shape))
            a = at[0]
            at[0] += n
            assert at[0] <= COLS, at[0]
            v = big[:, a:a + n]
            if len(shape) == 2:
                v = v.rearrange("p (a b) -> p a b", b=shape[1])
            if len(shape) == 3:
                v = v.rearrange("p (a b c) -> p a b c", b=shape[1], c=shape[2])
            return v

        win = cols(KD, PROJ)
        wout = cols(4, D)
        h = cols(CH, D)
        hT = cols(KD, SEQ)
        xc = cols(CB, SEQ)
        sz = cols(CH, INNER)
        xs = cols(INNER)
        xdt = cols(2, INNER)
        xdtd = cols(2, INNER)
        xsd = cols(2, INNER)
        bg = cols(2, 2 * P)
        gm = cols(2, P)
        mda = cols(2, HEADS * P)
        em = cols(2, HEADS * P)
        yb = cols(2, INNER)
        yTs = cols(4, P)
        st = cols(INNER)
        ab = cols(D)
        junk_y = cols(INNER)
        SOON = at[0] // EXPERT
        wgate = cols(KD, INTER - REST)
        wup = cols(KD, INTER - REST)
        wlast = cols(KD, P)
        wdown = cols(JB, D)
        x = cols(SEQS * CH, D)
        h1 = cols(CH, D)
        h2T = cols(KD, SEQ)
        sg = cols(2, SEQ)
        hid = cols(JB, SEQ)
        xn = cols(CH, D)
        xnT = cols(KD, P)
        junk_h = cols(D)
        dec = cols(3, CH, HEADS)
        dtx, dta, dtu, dtd, dtr, dts, dts2, dtq, dtp, dtl, dtv, dA = (cols(CH, HEADS) for _ in range(12))
        st6 = cols(CH, 6)
        mv = cols(CH, 2)
        ve, rs, rr, t4a, t4b, cur_rs, ssy, ry, vy, ssh, rh, vh, ve2, rs2 = (cols(CH) for _ in range(14))
        cur_mv = cols(CH, 2)
        st6b = cols(CH, 6)
        mv2 = cols(CH, 2)
        late_end = at[0]

        at[0] = E * EXPERT
        moe_small = at[0]
        xg = cols(KD * P)
        xT = cols(KD, P)
        sa = cols(2, HALF)
        ha = cols(MB, P)
        hTs = cols(MB, P)
        ys = cols(D)
        at[0] = max(at[0], late_end)
        cst = cols(N_CONST)
        vec = cols(N_VEC)
        wr = cols(KD, E)
        aneg = cols(HEADS)
        zero = cols(D)
        lg, rd, re_, rp, req, rsc, o1, o2, rq, sel, rpos, radr, rt = (cols(CH, E) for _ in range(13))
        rmx, rsum, rrec, rm1, rm2, p1, p2, ps12, pr12 = (cols(CH) for _ in range(9))
        rec = cols(CH, TOP, 2)
        slotf = cols(CH, TOP)
        slot = cols(CH, TOP).bitcast(I32)
        run = cols(E)
        full = cols(E, LIST)
        nt = cols(E)
        upto = cols(E)
        ge = cols(E)
        gn = cols(E)
        ecol = cols(1)
        scol = cols(1)
        rcol = cols(1)
        ridx = cols(1).bitcast(I32)
        ge_row = cols(TILES, E)
        erowf = cols(TILES)
        erow = cols(TILES).bitcast(I32)
        recg = cols(2 * P)
        rec0 = cols(2)
        ids = cols(TILES).bitcast(I32)
        wts = cols(TILES)
        gidx = cols(1).bitcast(I32)
        sidx = cols(1).bitcast(I32)

        ident = cst[:, C_ID:C_ID + P]
        tri_upto = cst[:, C_UPTO:C_UPTO + P]
        tri_after = cst[:, C_AFTER:C_AFTER + P]
        tri_before = cst[:, C_BEFORE:C_BEFORE + P]
        ones = cst[:, C_ONES:C_ONES + P]

        def expert_cols(e, off, n):
            return big[:, bass.ds(e * EXPERT + off, n)]

        ps = ctx.enter_context(nc.psum_tensor("ps", [P, 8 * 512], F32))

        def bank(k, n=1):
            return ps[:, k * 512:(k + n) * 512]

        small_in, win_in, wout_in, wout_scaled, rest_in, x_first, x_rest = map(sem, ("small_in", "win_in", "wout_in", "wout_scaled", "rest_in", "x_first", "x_rest"))
        early_in, expert_in, lists_in, zeroed, pads_out = map(sem, ("early_in", "expert_in", "lists_in", "zeroed", "pads_out"))
        aneg_exp, aneg_ready, run_zero = map(sem, ("aneg_exp", "aneg_ready", "run_zero"))
        ln1_var, ln1_r, h_ready, hT_ps, hT0_taken, hT1_taken = map(sem, ("ln1_var", "ln1_r", "h_ready", "hT_ps", "hT0_taken", "hT1_taken"))
        cur_kept = sem("cur_kept")
        dt_ps, dt_taken, dt_abs, dt_exp, dA_ready, dec_ps, dec_taken = map(sem, ("dt_ps", "dt_taken", "dt_abs", "dt_exp", "dA_ready", "dec_ps", "dec_taken"))
        xbc_ps, tap_done, conv_taken, xc_ready = map(sem, ("xbc_ps", "tap_done", "conv_taken", "xc_ready"))
        z_ps, z_taken = map(sem, ("z_ps", "z_taken"))
        xs_ps, xs_taken, bg_ps, bg_taken, seg_ps, seg_taken = map(sem, ("xs_ps", "xs_taken", "bg_ps", "bg_taken", "seg_ps", "seg_taken"))
        mda_ready, xdt_ready, xdtd_ready, xsd_ready, em_ready = map(sem, ("mda_ready", "xdt_ready", "xdtd_ready", "xsd_ready", "em_ready"))
        off_ps, off_scaled, y_ps, y_taken, s_ps, s_taken, y3_ready, y4_ready, ssy_ready, ry_ready = map(sem, ("off_ps", "off_scaled", "y_ps", "y_taken", "s_ps", "s_taken", "y3_ready", "y4_ready", "ssy_ready", "ry_ready"))
        yT_ps, yT_taken, o_ps, o_taken, xh_ready, ssh_ready, rh_ready = map(sem, ("yT_ps", "yT_taken", "o_ps", "o_taken", "xh_ready", "ssh_ready", "rh_ready"))
        h2_ready, h2T_ps, h2T0_taken, h2T1_taken = map(sem, ("h2_ready", "h2T_ps", "h2T0_taken", "h2T1_taken"))
        gate_ps, gate_taken, up_ps, up_taken, down_ps, down_taken = map(sem, ("gate_ps", "gate_taken", "up_ps", "up_taken", "down_ps", "down_taken"))
        ln2_var, ln2_r, xn_ready, xn_out, x1_out = map(sem, ("ln2_var", "ln2_r", "xn_ready", "xn_out", "x1_out"))
        xnT_ps, xnT_taken, lg_ps, lg_taken = map(sem, ("xnT_ps", "xnT_taken", "lg_ps", "lg_taken"))
        route_d, route_e, sel_ready, pos_ps, pos_taken, rec_ready, rec_out = map(sem, ("route_d", "route_e", "sel_ready", "pos_ps", "pos_taken", "rec_ready", "rec_out"))
        ridx_ready, erow_ready, recg_in, rec0_in, recT_ps, ids_ready = map(sem, ("ridx_ready", "erow_ready", "recg_in", "rec0_in", "recT_ps", "ids_ready"))
        gidx_ready, sidx_ready, xg_in, xT_ps, xT_taken = map(sem, ("gidx_ready", "sidx_ready", "xg_in", "xT_ps", "xT_taken"))
        a_ps, a_taken, b_ps, b_taken, eT_ps, eT0_taken, eT1_taken, yd_ps, yd_taken, y_added = map(sem, ("a_ps", "a_taken", "b_ps", "b_taken", "eT_ps", "eT0_taken", "eT1_taken", "yd_ps", "yd_taken", "y_added"))
        ln1_step, dt_step, conv_step, gm_step, s_step, a_step, ln2_step, route_step, half_step, table_step = map(sem, ("ln1_step", "dt_step", "conv_step", "gm_step", "s_step", "a_step", "ln2_step", "route_step", "half_step", "table_step"))
        pool_ln1, pool_ry, pool_rh = map(sem, ("pool_ln1", "pool_ry", "pool_rh"))

        ALL = slice(0, CH)
        HALVES = ((SEQS - 1, slice(0, CH // 2)), (SEQS, slice(CH // 2, CH)))

        def over_seqs(eng, body):
            body(0, False, True)
            with eng.Fori(1, SEQS - 1) as b:
                body(b, True, True)
            body(SEQS - 1, True, False)

        block = ctx.enter_context(nc.Block())

        @block.sync
        def _(sp):
            xv = hidden.rearrange("(t p) d -> p t d", p=P)
            sp.dma_start(x[:, 0:CH, :], xv[:, 0:CH, :]).then_inc(x_first, 16)
            sp.dma_start(cst, consts).then_inc(small_in, 16)
            sp.dma_start(vec, vecs).then_inc(small_in, 16)
            sp.dma_start(win, in_proj.rearrange("(k p) n -> p k n", p=P)).then_inc(win_in, 16)
            sp.dma_start(wout, out_proj.rearrange("(k p) n -> p k n", p=P)).then_inc(wout_in, 16)
            sp.dma_start(x[:, CH:, :], xv[:, CH:, :]).then_inc(x_rest, 16)
            for w, full_part, half_part in ((gate_w, wgate, 0), (up_w, wup, REST)):
                w = w.rearrange("(k p) n -> p k n", p=P)
                sp.dma_start(full_part, w[:, :, 0:INTER - REST]).then_inc(rest_in, 16)
                sp.dma_start(wlast[:, :, half_part:half_part + REST], w[:, :, INTER - REST:INTER]).then_inc(rest_in, 16)
            sp.dma_start(wdown[:, 0:JB - 1, :], down_w[0:(JB - 1) * P, :].rearrange("(k p) n -> p k n", p=P)).then_inc(rest_in, 16)
            sp.dma_start(wdown[P - REST:P, JB - 1, :], down_w[(JB - 1) * P:INTER, :]).then_inc(rest_in, 16)
            sp.dma_start(wr, router_w.rearrange("(k p) n -> p k n", p=P)).then_inc(rest_in, 16)
            sp.dma_start(lists, empty).then_inc(lists_in, 16)
            sp.wait_ge(zeroed, 1)
            sp.dma_start(xn_rows[TOKENS:, :], zero).then_inc(pads_out, 16)
            sp.dma_start(out[TOKENS:, :], zero).then_inc(pads_out, 16)

            def load_expert(e, done):
                a = e * EXPERT
                for w, off in ((w1, 0), (w3, KD * M)):
                    sp.dma_start(big[:, a + off:a + off + KD * M].rearrange("p (k n) -> p k n", k=KD),
                                 w[e].rearrange("(k p) n -> p k n", p=P)).then_inc(done, 16)
                sp.dma_start(big[:, a + 2 * KD * M:a + EXPERT].rearrange("p (k n) -> p k n", k=MB),
                             w2[e].rearrange("(k p) n -> p k n", p=P)).then_inc(done, 16)

            def load_next(e):
                if e > EARLY:
                    sp.wait_ge(expert_in, 48 * (e - EARLY))
                load_expert(e, expert_in)

            for e in range(EARLY):
                load_expert(e, early_in)
            x1_rows = out[0:TOKENS, :].rearrange("(t p) d -> p t d", p=P)
            xn_tiles = xn_rows[0:TOKENS, :].rearrange("(t p) d -> p t d", p=P)

            def body(b, prev, nxt):
                sp.wait_ge(down_taken, nth(b, CH, CH - 1))
                sp.dma_start(x1_rows[:, bass.ds(b * CH, CH), :], x[:, bass.ds(b * CH, CH), :]).then_inc(x1_out, 16)
                sp.wait_ge(xn_ready, nth(b, 1, 0) if nxt else SEQS + 1)
                sp.dma_start(xn_tiles[:, bass.ds(b * CH, CH), :], xn).then_inc(xn_out, 16)

            body(0, False, True)
            with sp.Fori(1, SEQS - 1) as b:
                body(b, True, True)
            sp.wait_ge(o_taken, SEQS * CH)
            sp.wait_ge(ssy_ready, SEQS * CH)
            for e in range(EARLY, SOON):
                load_next(e)
            body(SEQS - 1, True, False)
            sp.wait_ge(x1_out, 16 * SEQS)
            sp.wait_ge(xn_out, 16 * SEQS)
            sp.wait_ge(lg_ps, SEQS + 1)
            sp.wait_ge(rec_out, 16 * CH * TOP * SEQS)
            sp.dma_start(rec0, lists[0:P, :]).then_inc(rec0_in, 16)
            sp.wait_ge(xg_in, 16 * 2)
            for e in range(SOON, E):
                load_next(e)
            sp.wait_ge(pads_out, 32)
            sp.wait_ge(lists_in, 16)

        @block.tensor
        def _(pe):
            mm = nc.tensor.matmul

            def transposed(out_ap, in_ap, n=P):
                return nc.tensor.transpose(out_ap, in_ap, ident[0:n, 0:n])

            def hT_(n):
                pe.wait_ge(h_ready, nth(n, 1, 0))
                for k in range(KD):
                    for t in range(CH):
                        last = transposed(bank(2 + k)[:, t * P:(t + 1) * P], h[:, t, k * P:(k + 1) * P])
                    last.then_inc(hT_ps, 1)

            def dt_(n):
                pe.wait_ge(hT0_taken, nth(n, 1, 0))
                pe.wait_ge(hT1_taken, nth(n, 1, 0))
                for t in range(CH):
                    for k in range(KD):
                        last = mm(bank(1)[:, t * HEADS:(t + 1) * HEADS], hT[:, k, t * P:(t + 1) * P],
                                  win[:, k, PROJ - HEADS:PROJ], start=(k == 0), stop=(k == KD - 1))
                last.then_inc(dt_ps, 1)

            def dec_(n):
                pe.wait_ge(dA_ready, nth(n, 1, 0))
                for i, tri in enumerate((tri_after, tri_upto, ones)):
                    last = mm(bank(1)[:, i * CH * HEADS:(i + 1) * CH * HEADS], tri,
                              dA.rearrange("p a b -> p (a b)"), start=True, stop=True)
                last.then_inc(dec_ps, 1)

            def xbc_(n, j):
                if j >= 2:
                    pe.wait_ge(conv_taken, nth(n, CB, j - 2))
                for k in range(KD):
                    last = mm(bank(4 + j % 2), win[:, k, INNER + j * P:INNER + (j + 1) * P], hT[:, k, :],
                              start=(k == 0), stop=(k == KD - 1))
                last.then_inc(xbc_ps, 1)

            def z_(b, t):
                if t >= 2:
                    pe.wait_ge(z_taken, nth(b, CH, t - 2))
                elif t == 1:
                    pe.wait_ge(dec_taken, nth(b, 1, 0))
                for k in range(KD):
                    last = mm(bank(t % 2), hT[:, k, t * P:(t + 1) * P], win[:, k, 0:INNER],
                              start=(k == 0), stop=(k == KD - 1))
                last.then_inc(z_ps, 1)

            def front(b, c, prev):
                l = slice(c * P, (c + 1) * P)
                if c == 0:
                    pe.wait_ge(xc_ready, nth(b, CB, CB - 1))
                    if prev:
                        pe.wait_ge(gate_taken, b * JB)
                        pe.wait_ge(up_taken, b * JB)
                else:
                    pe.wait_ge(xs_taken, nth(b, CH, c - 1))
                for j in range(4):
                    last = transposed(bank(2)[:, j * P:(j + 1) * P], xc[:, j, l])
                last.then_inc(xs_ps, 1)
                if c > 0:
                    pe.wait_ge(bg_taken, nth(b, CH, c - 1))
                transposed(bank(3)[:, 0:P], xc[:, 4, l])
                mm(bank(3)[:, P:2 * P], xc[:, 4, l], xc[:, 5, l], start=True, stop=True).then_inc(bg_ps, 1)

            def seg_(b, c, prev):
                pe.wait_ge(mda_ready, nth(b, CH, c))
                if c > 0:
                    pe.wait_ge(seg_taken, nth(b, CH, c - 1))
                elif prev:
                    pe.wait_ge(down_taken, b * CH)
                for i in range(2):
                    last = mm(bank(4 + i), tri_after, mda[:, c % 2, i * 512:(i + 1) * 512], start=True, stop=True)
                last.then_inc(seg_ps, 1)

            def back(b, c, prev):
                l = slice(c * P, (c + 1) * P)
                if c == 0:
                    if prev:
                        pe.wait_ge(h2T0_taken, b)
                        pe.wait_ge(h2T1_taken, b)
                else:
                    pe.wait_ge(y_taken, nth(b, CH, c - 1))
                    pe.wait_ge(s_taken, nth(b, CH - 1, c - 1))
                    mm(bank(7), xc[:, 5, l], st, start=True, stop=True).then_inc(off_ps, 1)
                pe.wait_ge(em_ready, nth(b, CH, c))
                pe.wait_ge(xdt_ready, nth(b, CH, c))
                for hh in range(HEADS):
                    last = mm(bank(6)[:, hh * HD:(hh + 1) * HD], em[:, c % 2, hh * P:(hh + 1) * P],
                              xdt[:, c % 2, hh * HD:(hh + 1) * HD], start=True, stop=True)
                last.then_inc(y_ps, 1)
                if c < CH - 1:
                    pe.wait_ge(xdtd_ready, nth(b, CH - 1, c))
                    if c == 0 and not prev:
                        pe.wait_ge(z_taken, CH)
                    mm(bank(1), bg[:, c % 2, 0:P], xdtd[:, c % 2, :], start=True, stop=True).then_inc(s_ps, 1)

            def yT_(b, c):
                pe.wait_ge(y4_ready, nth(b, CH, c))
                if c > 0:
                    pe.wait_ge(o_taken, nth(b, CH, c - 1))
                for j in range(4):
                    last = transposed(bank(0)[:, j * P:(j + 1) * P], yb[:, c % 2, j * P:(j + 1) * P])
                last.then_inc(yT_ps, 1)

            def out_(b, c):
                pe.wait_ge(yT_taken, nth(b, CH, c))
                if isinstance(b, int) and b == 0 and c == 0:
                    pe.wait_ge(wout_scaled, 1)
                for k in range(4):
                    last = mm(bank(0)[:, 0:D], yTs[:, k, :], wout[:, k, :], start=(k == 0), stop=(k == 3))
                last.then_inc(o_ps, 1)

            def xnT_(n, t, b):
                if t == 0:
                    pe.wait_ge(xn_ready, nth(n, 1, 0))
                if t < CH - 1:
                    pe.wait_ge(xs_taken, nth(b, CH, t + 1))
                for k in range(KD):
                    last = transposed(bank(2)[:, k * P:(k + 1) * P], xn[:, t, k * P:(k + 1) * P])
                last.then_inc(xnT_ps, 1)

            def logits(n, t, b):
                pe.wait_ge(xnT_taken, nth(n, CH, t))
                pe.wait_ge(bg_taken, nth(b, CH, min(t + 1, CH - 1)))
                for k in range(KD):
                    last = mm(bank(3)[:, D + t * E:D + (t + 1) * E], xnT[:, k, :], wr[:, k, :], start=(k == 0), stop=(k == KD - 1))
                if t == CH - 1:
                    last.then_inc(lg_ps, 1)

            def positions(n, ts=ALL):
                pe.wait_ge(sel_ready, nth(n, 1, 0))
                s = sel[:, ts, :].rearrange("p a b -> p (a b)")
                to = slice(ts.start * E, ts.stop * E)
                mm(bank(6)[:, to], tri_before, s, start=True, stop=True)
                mm(bank(6)[:, CH * E:][:, to], ones, s, start=True, stop=True).then_inc(pos_ps, 1)

            def turn_half(part):
                n, ts = HALVES[part]
                pe.wait_ge(xn_ready, n + 1)
                if part == 1:
                    pe.wait_ge(xnT_taken, (SEQS - 1) * CH + 1)
                for k in range(KD):
                    for t in range(ts.start, ts.stop):
                        last = transposed(bank(2 + k)[:, t * P:(t + 1) * P], xn[:, t, k * P:(k + 1) * P])
                last.then_inc(xnT_ps, 1)

            def half_logits(part):
                n, ts = HALVES[part]
                pe.wait_ge(xnT_taken, (SEQS - 1) * CH + 1 + part)
                for t in range(ts.start, ts.stop):
                    for k in range(KD):
                        last = mm(bank(part)[:, t * E:(t + 1) * E], h2T[:, k, t * P:(t + 1) * P], wr[:, k, :],
                                  start=(k == 0), stop=(k == KD - 1))
                last.then_inc(lg_ps, 1)

            def mlp_up(b, j, nxt):
                if isinstance(b, int) and b == 0 and j == 0:
                    pe.wait_ge(rest_in, 16 * 7)
                bk = 2 * (j % 2)
                if j == 0:
                    pe.wait_ge(h2T0_taken, nth(b, 1, 0))
                    pe.wait_ge(h2T1_taken, nth(b, 1, 0))
                    pe.wait_ge(o_taken, nth(b, CH, CH - 1))
                    if nxt:
                        pe.wait_ge(z_taken, nth(b + 1, CH, CH - 1))
                elif j >= 2:
                    pe.wait_ge(gate_taken, nth(b, JB, j - 2))
                if j == JB - 1:
                    pe.wait_ge(up_taken, nth(b, JB, j - 2))
                    for k in range(KD):
                        last = mm(bank(bk), wlast[:, k, :], h2T[:, k, :], start=(k == 0), stop=(k == KD - 1))
                    last.then_inc(gate_ps, 1)
                    return
                for k in range(KD):
                    last = mm(bank(bk), wgate[:, k, j * P:(j + 1) * P], h2T[:, k, :], start=(k == 0), stop=(k == KD - 1))
                last.then_inc(gate_ps, 1)
                if j >= 2:
                    pe.wait_ge(up_taken, nth(b, JB, j - 2))
                for k in range(KD):
                    last = mm(bank(bk + 1), wup[:, k, j * P:(j + 1) * P], h2T[:, k, :], start=(k == 0), stop=(k == KD - 1))
                last.then_inc(up_ps, 1)

            def mlp_down(b, t):
                if t == 0:
                    pe.wait_ge(up_taken, nth(b, JB, JB - 2))
                if t >= 2:
                    pe.wait_ge(down_taken, nth(b, CH, t - 2))
                for j in range(JB):
                    q = slice(0, P) if j < JB - 1 else slice(P - REST, P)
                    if t == 0 and j == JB - 1:
                        pe.wait_ge(up_taken, nth(b, JB, j))
                    last = mm(bank(4 + t % 2)[:, 0:D], hid[q, j, t * P:(t + 1) * P], wdown[q, j, :],
                              start=(j == 0), stop=(j == JB - 1))
                last.then_inc(down_ps, 1)

            pe.wait_ge(small_in, 32)
            hT_(0)
            pe.wait_ge(win_in, 16)
            dt_(0)
            xbc_(0, 0)
            xbc_(0, 1)
            pe.wait_ge(dt_taken, 1)
            dec_(0)
            for t in range(CH):
                xbc_(0, t + 2)
                z_(0, t)
            pe.wait_ge(conv_taken, CB)

            def body(b, prev, nxt):
                seg_(b, 0, prev)
                front(b, 0, prev)
                for c in range(CH):
                    if c + 1 < CH:
                        seg_(b, c + 1, prev)
                    if prev and c > 0:
                        logits(b - 1, c - 1, b)
                    if c + 1 < CH:
                        front(b, c + 1, prev)
                    if c > 0:
                        yT_(b, c - 1)
                    if prev and c > 0:
                        xnT_(b - 1, c, b)
                    back(b, c, prev)
                    if prev and c == 0:
                        xnT_(b - 1, c, b)
                    if c > 0:
                        out_(b, c - 1)
                if prev:
                    logits(b - 1, CH - 1, b)
                if prev:
                    pe.wait_ge(lg_taken, b)
                if nxt:
                    pe.wait_ge(bg_taken, nth(b, CH, CH - 1))
                    hT_(b + 1)
                yT_(b, CH - 1)
                if nxt:
                    pe.wait_ge(s_taken, nth(b, CH - 1, CH - 2))
                    dt_(b + 1)
                    pe.wait_ge(seg_taken, nth(b, CH, CH - 1))
                    xbc_(b + 1, 0)
                out_(b, CH - 1)
                if nxt:
                    xbc_(b + 1, 1)
                    pe.wait_ge(dt_taken, nth(b, 1, 1))
                    dec_(b + 1)
                    pe.wait_ge(o_taken, nth(b, CH, CH - 1))
                    z_(b + 1, 0)
                    z_(b + 1, 1)
                    xbc_(b + 1, 2)
                    xbc_(b + 1, 3)
                    z_(b + 1, 2)
                    z_(b + 1, 3)
                pe.wait_ge(h2_ready, nth(b, 1, 0))
                pe.wait_ge(y_taken, nth(b, CH, CH - 1))
                for k in range(KD):
                    for t in range(CH):
                        last = transposed(bank(6 + k)[:, t * P:(t + 1) * P], h1[:, t, k * P:(k + 1) * P])
                    last.then_inc(h2T_ps, 1)
                if nxt:
                    xbc_(b + 1, 4)
                    xbc_(b + 1, 5)
                else:
                    pe.wait_ge(s_taken, nth(b, CH - 1, CH - 2))
                    pe.wait_ge(bg_taken, nth(b, CH, CH - 1))
                    pe.wait_ge(seg_taken, nth(b, CH, CH - 1))
                for j in range(JB):
                    mlp_up(b, j, nxt)
                    if prev and j == 3:
                        positions(b - 1)
                if nxt:
                    pe.wait_ge(conv_taken, nth(b + 1, CB, CB - 1))
                for t in range(CH):
                    mlp_down(b, t)
                if not nxt:
                    turn_half(0)
                    half_logits(0)

            over_seqs(pe, body)
            pe.wait_ge(gate_taken, SEQS * JB)
            pe.wait_ge(down_taken, SEQS * CH)
            turn_half(1)
            half_logits(1)
            for n, ts in HALVES:
                pe.wait_ge(pos_taken, n)
                positions(n, ts)

            pe.wait_ge(recg_in, 16)
            for i in range(2):
                last = transposed(bank(7)[:, i * TILES:(i + 1) * TILES],
                                  recg[0:TILES, :].rearrange("t (s two) -> t two s", two=2)[:, i, :], TILES)
            last.then_inc(recT_ps, 1)

            pe.wait_ge(erow_ready, 1)
            pe.wait_ge(ids_ready, 1)
            pe.wait_ge(early_in, 48 * EARLY)

            def xT_(i):
                pe.wait_ge(xg_in, 16 * (i + 1))
                for k in range(KD):
                    last = transposed(bank(6)[:, k * P:(k + 1) * P], xg[:, k * P:(k + 1) * P])
                last.then_inc(xT_ps, 1)

            def up(e, off, bk, done):
                for k in range(KD):
                    for n in range(2):
                        last = mm(bank(bk + n)[:, 0:HALF], xT[:, k, :], expert_cols(e, off + k * M + n * HALF, HALF),
                                  start=(k == 0), stop=(k == KD - 1))
                last.then_inc(done, 1)

            def hT_turn(i):
                pe.wait_ge(b_taken, i + 1)
                for j in range(MB):
                    last = transposed(bank(4, 2)[:, j * P:(j + 1) * P], ha[:, j, :])
                last.then_inc(eT_ps, 1)

            def down(i, first=False):
                e = pe.value_load(erow[0:1, bass.ds(i, 1)], min_val=0, max_val=E - 1)
                pe.wait_ge(eT0_taken, i + 1)
                pe.wait_ge(eT1_taken, i + 1)
                if not first:
                    pe.wait_ge(yd_taken, i)
                for j in range(MB):
                    last = mm(bank(7)[:, 0:D], hTs[:, j, :], expert_cols(e, 2 * KD * M + j * D, D),
                              start=(j == 0), stop=(j == MB - 1))
                last.then_inc(yd_ps, 1)

            def tile(i, prev, nxt, second=False):
                e = pe.value_load(erow[0:1, bass.ds(i, 1)], min_val=0, max_val=E - 1)
                pe.wait_ge(xT_taken, i + 1)
                if prev:
                    pe.wait_ge(a_taken, i)
                up(e, 0, 0, a_ps)
                if prev:
                    hT_turn(i - 1)
                up(e, KD * M, 2, b_ps)
                if nxt:
                    xT_(i + 1)
                if prev:
                    down(i - 1, second)

            xT_(0)
            tile(0, False, True)
            tile(1, True, True, True)
            with pe.Fori(EARLY, E) as i:
                pe.wait_ge(expert_in, 48 * (i - (EARLY - 1)))
                tile(i, True, True)
            with pe.Fori(E, TILES - 1) as i:
                tile(i, True, True)
            tile(TILES - 1, True, False)
            hT_turn(TILES - 1)
            down(TILES - 1)

        @block.scalar
        def _(act):
            A = nc.scalar.activation

            act.wait_ge(small_in, 32)
            A(aneg, vec[:, V_ALOG:V_ALOG + HEADS], ACT.Exp).then_inc(aneg_exp, 1)

            def hT0(n):
                act.wait_ge(hT_ps, nth(n, 2, 0))
                A(hT[:, 0, :], bank(2), ACT.Copy, scale=vec[:, V_N1:V_N1 + 1]).then_inc(hT0_taken, 1)

            def dt_e(n):
                act.wait_ge(dt_abs, nth(n, 1, 0))
                A(dtu, dta, ACT.Exp, scale=-1.0).then_inc(dt_exp, 1)

            def dec_e(n):
                act.wait_ge(dec_ps, nth(n, 1, 0))
                A(dec.rearrange("p a b c -> p (a b c)"), bank(1)[:, 0:3 * CH * HEADS], ACT.Exp).then_inc(dec_taken, 1)

            def tap(n, j):
                act.wait_ge(xbc_ps, nth(n, CB, j))
                w = V_CW + j * TAPS + TAPS - 1
                A(xc[:, j, :], bank(4 + j % 2), ACT.Identity, scale=vec[:, w:w + 1],
                  bias=vec[:, V_CB + j:V_CB + j + 1]).then_inc(tap_done, 1)

            def conv_silu(n, j):
                act.wait_ge(conv_taken, nth(n, CB, j))
                A(xc[:, j, :], xc[:, j, :], ACT.Silu).then_inc(xc_ready, 1)

            def decay(b, c):
                act.wait_ge(seg_ps, nth(b, CH, c))
                A(em[:, c % 2, :], bank(4, 2), ACT.Exp).then_inc(seg_taken, 1)

            def front(b, c):
                act.wait_ge(xs_ps, nth(b, CH, c))
                if not (isinstance(b, int) and b == 0 and c == 0):
                    act.wait_ge(xdt_ready, b * CH + c)
                    act.wait_ge(xsd_ready, b * CH + c)
                A(xs, bank(2), ACT.Copy).then_inc(xs_taken, 1)
                act.wait_ge(bg_ps, nth(b, CH, c))
                A(bg[:, c % 2, :], bank(3)[:, 0:2 * P], ACT.Copy).then_inc(bg_taken, 1)

            def x_D(b, c):
                act.wait_ge(xs_taken, nth(b, CH, c))
                if not (isinstance(b, int) and b == 0 and c < 2):
                    act.wait_ge(y_taken, b * CH + c - 1)
                for hh in range(HEADS):
                    q = slice(hh * HD, (hh + 1) * HD)
                    last = A(xsd[:, c % 2, q], xs[:, q], ACT.Copy, scale=vec[:, V_D + hh:V_D + hh + 1])
                last.then_inc(xsd_ready, 1)


            def z_silu(b, t):
                act.wait_ge(z_ps, nth(b, CH, t))
                A(sz[:, t, :], bank(t % 2), ACT.Silu).then_inc(z_taken, 1)

            def yT_copy(b, c):
                act.wait_ge(yT_ps, nth(b, CH, c))
                A(yTs.rearrange("p a b -> p (a b)"), bank(0), ACT.Copy).then_inc(yT_taken, 1)

            def xnT_copy(n, t):
                act.wait_ge(xnT_ps, nth(n, CH, t))
                A(xnT.rearrange("p k n -> p (k n)"), bank(2)[:, 0:D], ACT.Copy).then_inc(xnT_taken, 1)

            def logits_copy(n):
                act.wait_ge(lg_ps, nth(n, 1, 0))
                A(lg.rearrange("p a b -> p (a b)"), bank(3)[:, D:D + CH * E], ACT.Copy).then_inc(lg_taken, 1)

            def square_y(b, c):
                act.wait_ge(y4_ready, nth(b, CH, c))
                A(junk_y, yb[:, c % 2, :], ACT.Square, accum_out=ssy[:, c:c + 1]).then_inc(ssy_ready, 1)

            def square_h(b, c):
                act.wait_ge(o_taken, nth(b, CH, c))
                if not (isinstance(b, int) and b == 0 and c == 0):
                    act.wait_ge(ssh_ready, b * CH + c)
                A(junk_h, h1[:, c, :], ACT.Square, accum_out=ssh[:, c:c + 1]).then_inc(ssh_ready, 1)

            def route_exp(n):
                act.wait_ge(route_d, nth(n, 1, 0))
                A(re_, rd, ACT.Exp).then_inc(route_e, 1)

            hT0(0)
            dt_e(0)
            tap(0, 0)
            tap(0, 1)
            dec_e(0)
            for t in range(CH):
                tap(0, t + 2)
                z_silu(0, t)
                conv_silu(0, t)
            conv_silu(0, CB - 2)
            conv_silu(0, CB - 1)

            def body(b, prev, nxt):
                decay(b, 0)
                front(b, 0)
                x_D(b, 0)
                for c in range(CH):
                    if c + 1 < CH:
                        decay(b, c + 1)
                        front(b, c + 1)
                    if c >= 1:
                        yT_copy(b, c - 1)
                    if prev:
                        xnT_copy(b - 1, c)
                    if c >= 1:
                        square_y(b, c - 1)
                    if c + 1 < CH:
                        x_D(b, c + 1)
                    if c >= 2:
                        square_h(b, c - 2)
                if prev:
                    logits_copy(b - 1)
                square_h(b, CH - 2)
                if nxt:
                    hT0(b + 1)
                yT_copy(b, CH - 1)
                if nxt:
                    dt_e(b + 1)
                if prev:
                    route_exp(b - 1)
                square_y(b, CH - 1)
                if nxt:
                    tap(b + 1, 0)
                    tap(b + 1, 1)
                square_h(b, CH - 1)
                if nxt:
                    dec_e(b + 1)
                    conv_silu(b + 1, 0)
                    z_silu(b + 1, 0)
                    z_silu(b + 1, 1)
                    tap(b + 1, 2)
                    conv_silu(b + 1, 1)
                    tap(b + 1, 3)
                    z_silu(b + 1, 2)
                    z_silu(b + 1, 3)
                act.wait_ge(h2T_ps, nth(b, 2, 0))
                A(h2T[:, 0, :], bank(6), ACT.Copy, scale=vec[:, V_N2:V_N2 + 1]).then_inc(h2T0_taken, 1)
                if nxt:
                    conv_silu(b + 1, 2)
                    tap(b + 1, 4)
                    conv_silu(b + 1, 3)
                    tap(b + 1, 5)
                for j in range(JB):
                    if nxt and j < 2:
                        conv_silu(b + 1, 4 + j)
                    act.wait_ge(gate_ps, nth(b, JB, j))
                    if j >= 2:
                        act.wait_ge(up_taken, nth(b, JB, j - 2))
                    src, dst = (slice(0, P), slice(0, P)) if j < JB - 1 else (slice(0, REST), slice(P - REST, P))
                    A(sg[dst, j % 2, :], bank(2 * (j % 2))[src, :], ACT.Silu).then_inc(gate_taken, 1)

            over_seqs(act, body)
            for part, (n, ts) in enumerate(HALVES):
                q = slice(ts.start * P, ts.stop * P)
                act.wait_ge(xnT_ps, (SEQS - 1) * CH + 1 + part)
                A(h2T[:, :, q], bank(2, 2).rearrange("p (k n) -> p k n", k=KD)[:, :, q], ACT.Copy).then_inc(xnT_taken, 1)
                act.wait_ge(lg_ps, n + 1)
                A(lg[:, ts, :].rearrange("p a b -> p (a b)"), bank(part)[:, ts.start * E:ts.stop * E], ACT.Copy).then_inc(lg_taken, 1)
                act.wait_ge(route_d, n + 1)
                A(re_[:, ts, :], rd[:, ts, :], ACT.Exp).then_inc(route_e, 1)

            def xT_copy(i):
                act.wait_ge(xT_ps, i + 1)
                A(xT.rearrange("p k n -> p (k n)"), bank(6)[:, 0:D], ACT.Copy).then_inc(xT_taken, 1)

            def turn_tail(i):
                act.wait_ge(eT_ps, i + 1)
                A(hTs[:, 4:MB, :].rearrange("p a b -> p (a b)"), bank(5)[:, 0:(MB - 4) * P], ACT.Copy).then_inc(eT1_taken, 1)

            def tile(i, prev, nxt):
                act.wait_ge(a_ps, i + 1)
                if prev:
                    act.wait_ge(b_taken, i)
                A(sa, bank(0, 2).rearrange("p (a b) -> p a b", a=2)[:, :, 0:HALF], ACT.Silu).then_inc(a_taken, 1)
                if prev:
                    turn_tail(i - 1)
                if nxt:
                    xT_copy(i + 1)

            xT_copy(0)
            tile(0, False, True)
            with act.Fori(1, TILES - 1) as i:
                tile(i, True, True)
            tile(TILES - 1, True, False)
            turn_tail(TILES - 1)

        @block.vector
        def _(v):
            V = nc.vector
            idle = cols(8)

            def pass_wait(k):
                V.memset(idle[:, k:k + 1], 0.0)

            ln1 = Steps(v, ln1_step, 2)
            dts_ = Steps(v, dt_step, 6 + SERIES)
            conv = Steps(v, conv_step, TAPS - 2)
            rt_ = Steps(v, route_step, 25)
            half_rt = Steps(v, half_step, 23)
            tab = Steps(v, table_step, 11)

            def ln1_stats(n):
                if isinstance(n, int) and n == 0:
                    v.wait_ge(x_first, 16)
                ln1.start(n)
                for t in range(CH):
                    last = V.bn_stats(st6[:, t, :], x[:, bass.ds(n * CH + t, 1), :].rearrange("p a d -> p (a d)"))
                ln1.then(last)
                pass_wait(0)
                for t in range(CH):
                    last = V.bn_aggr(mv[:, t, :], st6[:, t, :])
                ln1.then(last)
                ln1.end()
                V.tensor_scalar_add(ve, mv[:, :, 1], LN_EPS).then_inc(ln1_var, 1)

            def ln1_h(n):
                v.wait_ge(ln1_r, nth(n, 1, 0))
                for t in range(CH):
                    last = V.tensor_scalar(h[:, t, :], x[:, bass.ds(n * CH + t, 1), :].rearrange("p a d -> p (a d)"),
                                           mv[:, t, 0:1], rr[:, t:t + 1], ALU.subtract, ALU.mult)
                last.then_inc(h_ready, 1)

            def hT1(n):
                v.wait_ge(hT_ps, nth(n, 2, 1))
                V.tensor_scalar(hT[:, 1, :], bank(3), vec[:, V_N1 + 1:V_N1 + 2], None, ALU.mult).then_inc(hT1_taken, 1)

            def dt_abs_(n):
                v.wait_ge(dt_ps, nth(n, 1, 0))
                V.tensor_tensor(dtx, bank(1)[:, 0:CH * HEADS].rearrange("p (a b) -> p a b", b=HEADS),
                                vec[:, V_DTB:V_DTB + HEADS].unsqueeze(1).to_broadcast([P, CH, HEADS]), ALU.add).then_inc(dt_taken, 1)
                v.wait_ge(dt_taken, nth(n, 1, 0))
                V.scalar_tensor_tensor(dta, dtx, -1.0, dtx, ALU.mult, ALU.max).then_inc(dt_abs, 1)

            def dt_softplus(n):
                dts_.start(n)
                v.wait_ge(dt_exp, nth(n, 1, 0))
                dts_.then(V.tensor_scalar_add(dtd, dtu, 2.0))
                dts_.then(V.reciprocal(dtr, dtd))
                dts_.then(V.tensor_tensor(dts, dtu, dtr, ALU.mult))
                dts_.then(V.tensor_tensor(dts2, dts, dts, ALU.mult))
                last = V.tensor_scalar(dtq, dts2, 1.0 / (2 * SERIES + 1), None, ALU.mult)
                for k in range(SERIES - 1, 0, -1):
                    dts_.then(last)
                    last = V.scalar_tensor_tensor(dtq, dtq, 1.0 / (2 * k + 1), dts2, ALU.add, ALU.mult)
                dts_.then(last)
                V.tensor_scalar(dtl, dtx, 0.0, None, ALU.max)
                dts_.then(V.scalar_tensor_tensor(dtp, dtq, 1.0, dts, ALU.add, ALU.mult))
                dts_.then(V.scalar_tensor_tensor(dtv, dtp, 2.0, dtl, ALU.mult, ALU.add))
                dts_.end()
                V.tensor_tensor(dA, dtv, aneg.unsqueeze(1).to_broadcast([P, CH, HEADS]), ALU.mult).then_inc(dA_ready, 1)

            def conv_taps(n, j):
                conv.start(n * CB + j)
                v.wait_ge(tap_done, nth(n, CB, j))
                for s in range(1, TAPS):
                    w = V_CW + j * TAPS + TAPS - 1 - s
                    last = V.scalar_tensor_tensor(xc[:, j, s:SEQ], bank(4 + j % 2)[:, 0:SEQ - s], vec[:, w:w + 1],
                                                  xc[:, j, s:SEQ], ALU.mult, ALU.add)
                    if s < TAPS - 1:
                        conv.then(last)
                conv.end()
                last.then_inc(conv_taken, 1)

            def heads(a):
                return a.rearrange("p (h q) -> p h q", h=HEADS)

            def over_head(a, n=HD):
                return a.unsqueeze(2).to_broadcast([P, HEADS, n])

            def front(b, c):
                v.wait_ge(bg_taken, nth(b, CH, c))
                V.tensor_tensor(gm[:, c % 2, :], bg[:, c % 2, P:2 * P], tri_upto, ALU.mult).then_inc(gm_step, 1)
                v.wait_ge(gm_step, nth(b, CH, c))
                v.wait_ge(seg_taken, nth(b, CH, c))
                V.tensor_tensor(heads(em[:, c % 2, :]), heads(em[:, c % 2, :]),
                                gm[:, c % 2, :].unsqueeze(1).to_broadcast([P, HEADS, P]), ALU.mult).then_inc(em_ready, 1)

            def off(b, c):
                v.wait_ge(off_ps, nth(b, CH - 1, c - 1))
                V.tensor_tensor(heads(yb[:, c % 2, :]), heads(bank(7)), over_head(dec[:, 1, c, :]), ALU.mult).then_inc(off_scaled, 1)
                if c < CH - 1:
                    V.tensor_tensor(heads(st), heads(st), over_head(dec[:, 2, c, :]), ALU.mult).then_inc(s_step, 1)

            def y_(b, c):
                v.wait_ge(y_ps, nth(b, CH, c))
                if c == 0:
                    v.wait_ge(xsd_ready, nth(b, CH, c))
                    V.tensor_tensor(yb[:, 0, :], xsd[:, 0, :], bank(6), ALU.add).then_inc(y_taken, 1)
                else:
                    v.wait_ge(y3_ready, nth(b, CH - 1, c - 1))
                    V.tensor_tensor(yb[:, c % 2, :], yb[:, c % 2, :], bank(6), ALU.add).then_inc(y_taken, 1)

            def state(b, c):
                if c == 0:
                    v.wait_ge(s_ps, nth(b, CH - 1, c))
                    V.tensor_copy(st, bank(1)).then_inc(s_taken, 1)
                elif c < CH - 1:
                    v.wait_ge(s_step, nth(b, CH - 2, c - 1))
                    v.wait_ge(s_ps, nth(b, CH - 1, c))
                    V.tensor_tensor(st, st, bank(1), ALU.add).then_inc(s_taken, 1)

            def decayed_x(b, c):
                v.wait_ge(xdt_ready, nth(b, CH, c))
                if c == 0:
                    v.wait_ge(dec_taken, nth(b, 1, 0))
                V.tensor_tensor(heads(xdtd[:, c % 2, :]), heads(xdt[:, c % 2, :]), over_head(dec[:, 0, c, :]), ALU.mult).then_inc(xdtd_ready, 1)

            def h1_(b, c):
                V.tensor_scalar(ab, x[:, bass.ds(b * CH + c, 1), :].rearrange("p a d -> p (a d)"),
                                cur_mv[:, c, 0:1], cur_rs[:, c:c + 1], ALU.subtract, ALU.mult).then_inc(a_step, 1)
                v.wait_ge(a_step, nth(b, CH, c))
                v.wait_ge(o_ps, nth(b, CH, c))
                v.wait_ge(ry_ready, nth(b, CH, c))
                V.scalar_tensor_tensor(h1[:, c, :], bank(0)[:, 0:D], ry[:, c:c + 1], ab, ALU.mult, ALU.add).then_inc(o_taken, 1)
                v.wait_ge(o_taken, nth(b, CH, c))
                xt = x[:, bass.ds(b * CH + c, 1), :].rearrange("p a d -> p (a d)")
                V.tensor_tensor(xt, xt, h1[:, c, :], ALU.add).then_inc(xh_ready, 1)

            def xn_(n, ts=ALL, seq=None):
                v.wait_ge(ln2_r, nth(n, 1, 0))
                seq = n if seq is None else seq
                if not (isinstance(seq, int) and seq == 0):
                    v.wait_ge(xn_out, 16 * seq)
                for t in range(ts.start, ts.stop):
                    last = V.tensor_scalar(xn[:, t, :], x[:, bass.ds(seq * CH + t, 1), :].rearrange("p a d -> p (a d)"),
                                           mv2[:, t, 0:1], rs2[:, t:t + 1], ALU.subtract, ALU.mult)
                last.then_inc(xn_ready, 1)

            def over_e(a, ts):
                return a[:, ts].unsqueeze(2).to_broadcast([P, ts.stop - ts.start, E])

            def over_t(a, ts):
                return a.unsqueeze(1).to_broadcast([P, ts.stop - ts.start, E])

            def route_max(n, ts=ALL, first=0, steps=rt_):
                steps.start(n - first)
                v.wait_ge(lg_taken, nth(n, 1, 0))
                steps.then(V.tensor_reduce(rmx[:, ts], lg[:, ts, :], AX, ALU.max))
                V.tensor_tensor(rd[:, ts, :], lg[:, ts, :], over_e(rmx, ts), ALU.subtract).then_inc(route_d, 1)

            def pick(p, most, o, m, ts, steps):
                steps.then(V.tensor_reduce(most[:, ts], p[:, ts, :], AX, ALU.max))
                steps.then(V.tensor_tensor(req[:, ts, :], p[:, ts, :], over_e(most, ts), ALU.is_equal))
                steps.then(V.tensor_tensor(rsc[:, ts, :], req[:, ts, :], over_t(cst[:, C_RANK:C_RANK + E], ts), ALU.mult))
                steps.then(V.tensor_reduce(m[:, ts], rsc[:, ts, :], AX, ALU.max))
                steps.then(V.tensor_tensor(o[:, ts, :], rsc[:, ts, :], over_e(m, ts), ALU.is_equal))

            def route_pick(n, ts=ALL, seq=None, steps=rt_):
                v.wait_ge(route_e, nth(n, 1, 0))
                steps.then(V.tensor_reduce(rsum[:, ts], re_[:, ts, :], AX, ALU.add))
                steps.then(V.reciprocal(rrec[:, ts], rsum[:, ts]))
                steps.then(V.tensor_tensor(rp[:, ts, :], re_[:, ts, :], over_e(rrec, ts), ALU.mult))
                pick(rp, p1, o1, rm1, ts, steps)
                steps.then(V.scalar_tensor_tensor(rq[:, ts, :], o1[:, ts, :], -2.0, rp[:, ts, :], ALU.mult, ALU.add))
                pick(rq, p2, o2, rm2, ts, steps)
                V.tensor_tensor(sel[:, ts, :], o1[:, ts, :], o2[:, ts, :], ALU.add).then_inc(sel_ready, 1)
                steps.then(V.tensor_tensor(ps12[:, ts], p1[:, ts], p2[:, ts], ALU.add))
                steps.then(V.reciprocal(pr12[:, ts], ps12[:, ts]))
                seq = n if seq is None else seq
                if not (isinstance(seq, int) and seq == 0):
                    v.wait_ge(rec_out, 16 * CH * TOP * seq)
                for k, p in enumerate((p1, p2)):
                    V.tensor_tensor(rec[:, ts, k, 1], p[:, ts], pr12[:, ts], ALU.mult)
                    V.tensor_copy(rec[:, ts, k, 0], cst[:, bass.ds(C_TOKEN + seq * CH + ts.start, ts.stop - ts.start)])

            def route_slots(n, ts=ALL, steps=rt_):
                v.wait_ge(pos_ps, nth(n, 1, 0))
                for t in range(ts.start, ts.stop):
                    V.tensor_tensor(rpos[:, t, :], bank(6)[:, t * E:(t + 1) * E], run, ALU.add)
                    last = V.tensor_tensor(run, run, bank(6)[:, (CH + t) * E:(CH + t + 1) * E], ALU.add)
                    if t < ts.stop - 1:
                        steps.then(last)
                last.then_inc(pos_taken, 1)
                v.wait_ge(pos_taken, nth(n, 1, 0))
                steps.then(V.tensor_tensor(radr[:, ts, :], rpos[:, ts, :], over_t(cst[:, C_LISTS:C_LISTS + E], ts), ALU.add))
                for k, o in enumerate((o1, o2)):
                    steps.then(V.tensor_tensor(rt[:, ts, :], o[:, ts, :], radr[:, ts, :], ALU.mult))
                    steps.then(V.tensor_reduce(slotf[:, ts, k], rt[:, ts, :], AX, ALU.add))
                V.tensor_copy(slot[:, ts, :], slotf[:, ts, :]).then_inc(rec_ready, 1)
                steps.end()

            def add_mlp(b, t):
                xt = x[:, bass.ds(b * CH + t, 1), :].rearrange("p a d -> p (a d)")
                v.wait_ge(down_ps, nth(b, CH, t))
                V.tensor_tensor(xt, xt, bank(4 + t % 2)[:, 0:D], ALU.add).then_inc(down_taken, 1)
                v.wait_ge(down_taken, nth(b, CH, t))
                pass_wait(1)
                V.bn_stats(st6b[:, t, :], xt).then_inc(ln2_step, 1)

            def ln2_stats(b, ts, bns, before=0):
                v.wait_ge(ln2_step, b * (CH + 1) + bns + before)
                pass_wait(2)
                for t in range(ts.start, ts.stop):
                    last = V.bn_aggr(mv2[:, t, :], st6b[:, t, :])
                last.then_inc(ln2_step, 1)
                v.wait_ge(ln2_step, b * (CH + 1) + bns + before + 1)
                V.tensor_scalar_add(ve2[:, ts], mv2[:, ts, 1], LN_EPS).then_inc(ln2_var, 1)

            V.memset(zero, 0.0).then_inc(zeroed, 1)
            V.memset(run, 0.0).then_inc(run_zero, 1)
            v.wait_ge(run_zero, 1)
            v.wait_ge(aneg_exp, 1)
            V.tensor_scalar(aneg, aneg, -1.0, None, ALU.mult).then_inc(aneg_ready, 1)
            v.wait_ge(aneg_ready, 1)
            ln1_stats(0)
            ln1_h(0)
            hT1(0)
            dt_abs_(0)
            dt_softplus(0)
            for j in range(CB):
                conv_taps(0, j)
            v.wait_ge(x_rest, 16)

            def body(b, prev, nxt):
                V.tensor_copy(cur_mv, mv)
                V.tensor_copy(cur_rs, rs).then_inc(cur_kept, 1)
                v.wait_ge(cur_kept, nth(b, 1, 0))
                front(b, 0)
                if prev:
                    xn_(b - 1)
                decayed_x(b, 0)
                for c in range(CH):
                    if c + 1 < CH:
                        front(b, c + 1)
                    if c >= 2:
                        v.wait_ge(yT_taken, nth(b, CH, c - 2))
                    if c > 0:
                        off(b, c)
                    y_(b, c)
                    state(b, c)
                    if c > 0:
                        h1_(b, c - 1)
                    if c + 1 < CH - 1:
                        decayed_x(b, c + 1)
                    if nxt and c == 0:
                        ln1_stats(b + 1)
                    if nxt and c == 2:
                        ln1_h(b + 1)
                if nxt:
                    hT1(b + 1)
                if prev:
                    route_max(b - 1)
                if nxt:
                    dt_abs_(b + 1)
                    dt_softplus(b + 1)
                h1_(b, CH - 1)
                if nxt:
                    conv_taps(b + 1, 0)
                    conv_taps(b + 1, 1)
                v.wait_ge(rh_ready, nth(b, 1, 0))
                v.wait_ge(xh_ready, nth(b, CH, CH - 1))
                for t in range(CH):
                    last = V.tensor_scalar(h1[:, t, :], h1[:, t, :], rh[:, t:t + 1], None, ALU.mult)
                last.then_inc(h2_ready, 1)
                if nxt:
                    conv_taps(b + 1, 2)
                    conv_taps(b + 1, 3)
                v.wait_ge(h2T_ps, nth(b, 2, 1))
                V.tensor_scalar(h2T[:, 1, :], bank(7), vec[:, V_N2 + 1:V_N2 + 2], None, ALU.mult).then_inc(h2T1_taken, 1)
                if nxt:
                    conv_taps(b + 1, 4)
                    conv_taps(b + 1, 5)
                for j in range(JB):
                    v.wait_ge(gate_taken, nth(b, JB, j))
                    if j < JB - 1:
                        v.wait_ge(up_ps, nth(b, JB - 1, j))
                        V.tensor_tensor(hid[:, j, :], sg[:, j % 2, :], bank(2 * (j % 2) + 1), ALU.mult).then_inc(up_taken, 1)
                    else:
                        q = slice(P - REST, P)
                        V.tensor_tensor(hid[q, j, :], sg[q, j % 2, :], bank(2 * (j % 2))[q, :], ALU.mult).then_inc(up_taken, 1)
                    if prev and j == 1:
                        route_pick(b - 1)
                    if prev and j == 4:
                        route_slots(b - 1)
                if nxt:
                    for t in range(CH):
                        add_mlp(b, t)
                    ln2_stats(b, ALL, CH)
                else:
                    for part, (n, ts) in enumerate(HALVES):
                        for t in range(ts.start, ts.stop):
                            add_mlp(b, t)
                            if t == CH - 2:
                                xn_(n - 1, HALVES[0][1], b)
                        ln2_stats(b, ts, ts.stop, part)

            over_seqs(v, body)
            for n, ts in HALVES:
                route_max(n, ts, SEQS - 1, half_rt)
                if n < SEQS:
                    xn_(SEQS, HALVES[1][1], SEQS - 1)
                route_pick(n, ts, SEQS - 1, half_rt)
                route_slots(n, ts, half_rt)

            tab.start(0)
            tab.then(V.tensor_tensor(full, run.unsqueeze(2).to_broadcast([P, E, LIST]),
                                     cst[:, C_FULL:C_FULL + LIST].unsqueeze(1).to_broadcast([P, E, LIST]), ALU.is_gt))
            tab.then(V.tensor_reduce(nt, full, AX, ALU.add))
            tab.then(V.tensor_scalar(nt, nt, 1.0, None, ALU.max))
            tab.then(V.tensor_tensor_scan(upto, ones[:, 0:E], nt, 0.0, ALU.mult, ALU.add))
            tab.then(V.tensor_scalar(ge[:, 0:E - 1], upto[:, 0:E - 1], cst[:, C_ROW:C_ROW + 1], None, ALU.is_le))
            tab.then(V.tensor_tensor(gn[:, 0:E - 1], ge[:, 0:E - 1], nt[:, 0:E - 1], ALU.mult))
            tab.then(V.tensor_reduce(scol, gn[:, 0:E - 1], AX, ALU.add))
            tab.then(V.tensor_reduce(ecol, ge[:, 0:E - 1], AX, ALU.add))
            tab.then(V.tensor_scalar(rcol, ecol, float(LIST), cst[:, C_ROW:C_ROW + 1], ALU.mult, ALU.add))
            V.tensor_tensor(ridx, rcol, scol, ALU.subtract).then_inc(ridx_ready, 1)
            tab.then(V.tensor_tensor(ge_row[0:1, :, 0:E - 1],
                                     upto[0:1, 0:E - 1].unsqueeze(1).to_broadcast([1, TILES, E - 1]),
                                     cst[0:1, C_TILE:C_TILE + TILES].unsqueeze(2).to_broadcast([1, TILES, E - 1]), ALU.is_le))
            tab.then(V.tensor_reduce(erowf[0:1, :], ge_row[0:1, :, 0:E - 1], AX, ALU.add))
            tab.end()
            V.tensor_copy(erow[0:1, :], erowf[0:1, :]).then_inc(erow_ready, 1)
            v.wait_ge(recT_ps, 1)
            V.tensor_copy(ids, bank(7)[:, 0:TILES])
            V.tensor_copy(wts, bank(7)[:, TILES:2 * TILES]).then_inc(ids_ready, 1)
            v.wait_ge(ids_ready, 1)

            def turn_head(i):
                v.wait_ge(eT_ps, i + 1)
                V.tensor_copy(hTs[:, 0:4, :].rearrange("p a b -> p (a b)"), bank(4)).then_inc(eT0_taken, 1)

            def weigh(i, first=False):
                v.wait_ge(yd_ps, i + 1)
                if not first:
                    v.wait_ge(y_added, 16 * i)
                V.tensor_scalar(ys, bank(7)[:, 0:D], wts[:, bass.ds(i, 1)], None, ALU.mult).then_inc(yd_taken, 1)

            def tile(i, prev, second=False):
                if prev:
                    turn_head(i - 1)
                v.wait_ge(b_ps, i + 1)
                v.wait_ge(a_taken, i + 1)
                V.tensor_tensor(ha.rearrange("p a b -> p (a b)").rearrange("p (a b) -> p a b", a=2), sa,
                                bank(2, 2).rearrange("p (a b) -> p a b", a=2)[:, :, 0:HALF], ALU.mult).then_inc(b_taken, 1)
                if prev:
                    weigh(i - 1, second)

            tile(0, False)
            tile(1, True, True)
            with v.Fori(2, TILES) as i:
                tile(i, True)
            turn_head(TILES - 1)
            weigh(TILES - 1)

        @block.gpsimd
        def _(g):
            G = nc.gpsimd
            idle = cols(8)

            def pass_wait(k):
                G.tensor_tensor(idle[:, k:k + 1], half[:, 0:1], half[:, 0:1], ALU.add)

            half = cst[:, C_POW:C_POW + 4]
            g_ln1 = Steps(g, pool_ln1, 4)

            def heads(a):
                return a.rearrange("p (h q) -> p h q", h=HEADS)

            def over_head(a, n=HD):
                return a.unsqueeze(2).to_broadcast([P, HEADS, n])

            def ln1_scale(n):
                g.wait_ge(ln1_var, nth(n, 1, 0))
                g_ln1.start(n)
                g_ln1.then(G.tensor_tensor(rs, ve, half, ALU.pow))
                g_ln1.then(G.tensor_tensor(t4a, rs, rs, ALU.mult))
                g_ln1.then(G.tensor_tensor(t4b, t4a, mv[:, :, 1], ALU.mult))
                pass_wait(0)

            def rms_scale(n):
                G.tensor_scalar(t4a, t4b, 1.0, RMS_EPS, ALU.mult, ALU.add).then_inc(pool_rh, 1)
                g.wait_ge(pool_rh, nth(n, 1, 0))
                g_ln1.then(G.tensor_tensor(t4b, t4a, half, ALU.pow))
                g_ln1.end()
                G.tensor_tensor(rr, rs, t4b, ALU.mult).then_inc(ln1_r, 1)

            def masked_dA(n, c):
                g.wait_ge(dA_ready, nth(n, 1, 0))
                if not (isinstance(n, int) and n == 0 and c < 2):
                    g.wait_ge(seg_ps, n * CH + c - 1)
                G.tensor_tensor(heads(mda[:, c % 2, :]), tri_upto.unsqueeze(1).to_broadcast([P, HEADS, P]),
                                over_head(dA[:, c, :], P), ALU.mult).then_inc(mda_ready, 1)

            def scaled_x(b, c):
                g.wait_ge(xs_taken, nth(b, CH, c))
                G.tensor_tensor(heads(xdt[:, c % 2, :]), heads(xs), over_head(dtv[:, c, :]), ALU.mult).then_inc(xdt_ready, 1)

            def plus_x_D(b, c):
                g.wait_ge(xsd_ready, nth(b, CH, c))
                g.wait_ge(off_scaled, nth(b, CH - 1, c - 1))
                G.tensor_tensor(yb[:, c % 2, :], yb[:, c % 2, :], xsd[:, c % 2, :], ALU.add).then_inc(y3_ready, 1)

            def gated(b, c):
                g.wait_ge(y_taken, nth(b, CH, c))
                if c == 0:
                    g.wait_ge(z_taken, nth(b, CH, CH - 1))
                G.tensor_tensor(yb[:, c % 2, :], yb[:, c % 2, :], sz[:, c, :], ALU.mult).then_inc(y4_ready, 1)

            def scale_y(b, c):
                g.wait_ge(ssy_ready, nth(b, CH, c))
                pass_wait(1)
                G.tensor_scalar(vy[:, c:c + 1], ssy[:, c:c + 1], 1.0 / INNER, RMS_EPS, ALU.mult, ALU.add).then_inc(pool_ry, 1)
                g.wait_ge(pool_ry, nth(b, CH + 1, c))
                G.tensor_tensor(ry[:, c:c + 1], vy[:, c:c + 1], half[:, 0:1], ALU.pow).then_inc(ry_ready, 1)

            def scatter(n, ts=ALL):
                g.wait_ge(lists_in, 16)
                g.wait_ge(rec_ready, nth(n, 1, 0))
                if not isinstance(n, int):
                    pass_wait(2)
                for t in range(ts.start, ts.stop):
                    for k in range(TOP):
                        G.indirect_dma_start(lists, bass.IndirectOffsetOnAxis(ap=slot[:, t, k:k + 1], axis=0),
                                             rec[:, t, k, :], None).then_inc(rec_out, 16)

            ln1_scale(0)
            rms_scale(0)
            g.wait_ge(wout_in, 16)
            for k in range(4):
                last = G.tensor_tensor(wout[:, k, :], wout[:, k, :], vec[:, V_MN + k:V_MN + k + 1].to_broadcast([P, D]), ALU.mult)
            last.then_inc(wout_scaled, 1)
            masked_dA(0, 0)
            masked_dA(0, 1)

            def body(b, prev, nxt):
                scaled_x(b, 0)
                for c in range(CH):
                    if c + 2 < CH:
                        masked_dA(b, c + 2)
                    if c + 1 < CH:
                        scaled_x(b, c + 1)
                    if c > 0:
                        plus_x_D(b, c)
                        scale_y(b, c - 1)
                    gated(b, c)
                    if nxt and c == 1:
                        ln1_scale(b + 1)
                    if nxt and c == 2:
                        rms_scale(b + 1)
                scale_y(b, CH - 1)
                g.wait_ge(ssh_ready, nth(b, CH, CH - 1))
                pass_wait(3)
                G.tensor_scalar(vh, ssh, 1.0 / D, RMS_EPS, ALU.mult, ALU.add).then_inc(pool_ry, 1)
                g.wait_ge(pool_ry, nth(b, CH + 1, CH))
                G.tensor_tensor(rh, vh, half, ALU.pow).then_inc(rh_ready, 1)
                if nxt:
                    masked_dA(b + 1, 0)
                    masked_dA(b + 1, 1)
                if prev:
                    scatter(b - 1)
                for n, ts in ([(b, ALL)] if nxt else HALVES):
                    g.wait_ge(ln2_var, nth(n, 1, 0))
                    G.tensor_tensor(rs2[:, ts], ve2[:, ts], half[:, ts], ALU.pow).then_inc(ln2_r, 1)

            over_seqs(g, body)
            for n, ts in HALVES:
                scatter(n, ts)
            g.wait_ge(rec_out, 16 * CH * TOP * SEQS)
            g.wait_ge(ridx_ready, 1)
            G.indirect_dma_start(recg[0:TILES, :], None, lists.rearrange("(t s) two -> t (s two)", s=P),
                                 bass.IndirectOffsetOnAxis(ap=ridx[0:TILES, :], axis=0)).then_inc(recg_in, 16)

            g.wait_ge(xn_out, 16 * SEQS)
            g.wait_ge(x1_out, 16 * SEQS)
            g.wait_ge(pads_out, 32)

            def gather(i, first=False):
                G.tensor_copy(gidx, rec0[:, 0:1] if first else ids[:, bass.ds(i, 1)]).then_inc(gidx_ready, 1)
                g.wait_ge(gidx_ready, i + 1)
                pass_wait(4)
                G.indirect_dma_start(xg, None, xn_rows, bass.IndirectOffsetOnAxis(ap=gidx, axis=0)).then_inc(xg_in, 16)

            def add_rows(i, first=False):
                g.wait_ge(yd_taken, i + 1)
                if not first:
                    g.wait_ge(y_added, 16 * i)
                    pass_wait(5)
                G.tensor_copy(sidx, ids[:, bass.ds(i, 1)]).then_inc(sidx_ready, 1)
                g.wait_ge(sidx_ready, i + 1)
                pass_wait(6)
                G.indirect_dma_start(out, bass.IndirectOffsetOnAxis(ap=sidx, axis=0), ys, None,
                                     compute_op=ALU.add, bounds_check=TOKENS + P - 1, oob_is_err=True).then_inc(y_added, 16)

            g.wait_ge(rec0_in, 16)
            gather(0, True)
            g.wait_ge(ids_ready, 1)
            g.wait_ge(xT_ps, 1)
            gather(1)
            g.wait_ge(xT_ps, 2)
            gather(2)
            add_rows(0, True)
            with g.Fori(1, TILES - 2) as i:
                g.wait_ge(xT_ps, i + 2)
                pass_wait(7)
                gather(i + 2)
                add_rows(i)
            add_rows(TILES - 2)
            add_rows(TILES - 1)
            g.wait_ge(y_added, 16 * TILES)


_VECTORS = ("L0_attn_norm1_w", "L0_attn_mixer_norm_w", "L0_attn_norm2_w")


def kernel(**inputs):
    import concourse.bacc as bacc
    from concourse.bass_utils import run_bass_kernel_spmd

    a = {k: np.asarray(v) for k, v in inputs.items()}

    def down_partitions(v):
        return v.reshape(-1, P).T

    def all_partitions(v):
        return np.broadcast_to(v[None, :], (P, v.shape[0]))

    conv_w = a["L0_attn_conv_w"].reshape(CB, P, TAPS).transpose(1, 0, 2).reshape(P, CB * TAPS)
    vecs = np.concatenate(
        [down_partitions(a[n]) for n in _VECTORS]
        + [conv_w, down_partitions(a["L0_attn_conv_b"])]
        + [all_partitions(a[n]) for n in ("L0_attn_dt_bias", "L0_attn_A_log", "L0_attn_D_param")], axis=1)
    consts, empty = constants()
    arrays = {
        "hidden": a["L0_attn_hidden_states"].reshape(TOKENS, D), "vecs": vecs, "consts": consts, "empty": empty,
        "in_proj": a["L0_attn_in_proj_w"], "out_proj": a["L0_attn_out_proj_w"], "gate": a["L0_attn_gate_w"],
        "up": a["L0_attn_up_w"], "down": a["L0_attn_down_w"], "router": a["L0_ffn_gate_w"],
        "w1": a["L0_ffn_w1"], "w2": a["L0_ffn_w2"], "w3": a["L0_ffn_w3"],
    }
    arrays = {f"in_{k}": np.ascontiguousarray(v) for k, v in arrays.items()}
    nc = bacc.Bacc("TRN2", target_bir_lowering=False, num_devices=1)
    args = [nc.dram_tensor(k, v.shape, mybir.dt.from_np(v.dtype), kind="ExternalInput").ap() for k, v in arrays.items()]
    out = nc.dram_tensor("out_rows", (TOKENS + P, D), F32, kind="ExternalOutput").ap()
    build(nc, *args, out)
    r = run_bass_kernel_spmd(nc, [arrays], core_ids=[0])
    return np.asarray(r.results[0]["out_rows"])[:TOKENS].reshape(SEQS, SEQ, D)
```
